# Optimizing a Trainium2 kernel written in Bass

```python
import numpy as np
import jax
import jax.numpy as jnp

def _softmax(x, axis=-1):
    return jax.nn.softmax(x, axis=axis)

def _gelu(x):
    return jax.nn.gelu(x, approximate=True)

def _silu(x):
    return jax.nn.silu(x)

def _sigmoid(x):
    return jax.nn.sigmoid(x)

def _layernorm(x, axis=-1, eps=1e-05):
    m = jnp.mean(x, axis=axis, keepdims=True)
    v = jnp.var(x, axis=axis, keepdims=True)
    return (x - m) / jnp.sqrt(v + eps)

def _scatter_add(tgt, idx, src, axis=0):
    return tgt.at[idx].add(src)

def _segment_sum(src, seg, n):
    return jax.ops.segment_sum(src, seg, n)
kernel_name = 'mk_seq_preln_d1_jaxref_r4_4055ed'

def setup_inputs(seed: int=0):
    np.random.seed(seed)
    _w = jnp.asarray

    def _L0_attn_setup():
        import jax, jax.numpy as jnp
        import numpy as np
        HEAD_NUM = 16
        ROPE_BASE = 10000.0

        def _rotate_half(x):
            x_even = x[..., ::2]
            x_odd = x[..., 1::2]
            return jnp.stack((-x_odd, x_even), axis=-1).reshape(x.shape)

        def _rope_cos_sin(seq_len, head_dim):
            half = head_dim // 2
            inv_freq = 1.0 / ROPE_BASE ** (jnp.arange(half, dtype=jnp.float32) / half)
            t = jnp.arange(seq_len, dtype=jnp.float32)
            freqs = t[:, None] * inv_freq[None, :]
            cos = jnp.repeat(jnp.cos(freqs), 2, axis=-1)
            sin = jnp.repeat(jnp.sin(freqs), 2, axis=-1)
            return (cos, sin)
        key = jax.random.key(seed)
        ks = jax.random.split(key, 9)
        B, S, H = (2, 512, 512)
        std = 1.0 / np.sqrt(H)
        return {'x': jax.random.normal(ks[0], (B, S, H), jnp.float32), 'Wq': jax.random.normal(ks[1], (H, H), jnp.float32) * std, 'bq': jax.random.normal(ks[2], (H,), jnp.float32) * std, 'Wk': jax.random.normal(ks[3], (H, H), jnp.float32) * std, 'bk': jax.random.normal(ks[4], (H,), jnp.float32) * std, 'Wv': jax.random.normal(ks[5], (H, H), jnp.float32) * std, 'bv': jax.random.normal(ks[6], (H,), jnp.float32) * std, 'Wo': jax.random.normal(ks[7], (H, H), jnp.float32) * std, 'bo': jax.random.normal(ks[8], (H,), jnp.float32) * std}
    _L0_attn_in = _L0_attn_setup()

    def _L0_ffn_setup():
        import jax, jax.numpy as jnp
        import numpy as np
        HIDDEN = 512
        INTER = 1408
        B, S = (2, 512)

        def _ternary(key, shape):
            return jax.random.randint(key, shape, -1, 2).astype(jnp.float32)
        key = jax.random.key(seed)
        ks = jax.random.split(key, 7)
        x = jax.random.normal(ks[0], (B, S, HIDDEN), dtype=jnp.float32)
        gate_w = _ternary(ks[1], (INTER, HIDDEN))
        up_w = _ternary(ks[2], (INTER, HIDDEN))
        down_w = _ternary(ks[3], (HIDDEN, INTER))
        gate_s = jax.random.uniform(ks[4], (INTER,), minval=0.01, maxval=0.1, dtype=jnp.float32)
        up_s = jax.random.uniform(ks[5], (INTER,), minval=0.01, maxval=0.1, dtype=jnp.float32)
        down_s = jax.random.uniform(ks[6], (HIDDEN,), minval=0.01, maxval=0.1, dtype=jnp.float32)
        return {'x': x, 'gate_w': gate_w, 'up_w': up_w, 'down_w': down_w, 'gate_s': gate_s, 'up_s': up_s, 'down_s': down_s}
    _L0_ffn_in = _L0_ffn_setup()
    _d = {'L0_attn_x': _L0_attn_in['x'], 'L0_attn_Wq': _L0_attn_in['Wq'], 'L0_attn_bq': _L0_attn_in['bq'], 'L0_attn_Wk': _L0_attn_in['Wk'], 'L0_attn_bk': _L0_attn_in['bk'], 'L0_attn_Wv': _L0_attn_in['Wv'], 'L0_attn_bv': _L0_attn_in['bv'], 'L0_attn_Wo': _L0_attn_in['Wo'], 'L0_attn_bo': _L0_attn_in['bo'], 'L0_ffn_gate_w': _L0_ffn_in['gate_w'], 'L0_ffn_up_w': _L0_ffn_in['up_w'], 'L0_ffn_down_w': _L0_ffn_in['down_w'], 'L0_ffn_gate_s': _L0_ffn_in['gate_s'], 'L0_ffn_up_s': _L0_ffn_in['up_s'], 'L0_ffn_down_s': _L0_ffn_in['down_s']}
    _x0 = _d['L0_attn_x']
    _d['L0_attn_x'] = jax.random.normal(jax.random.fold_in(jax.random.key(seed), 1), (2, 1024, 512), dtype=_x0.dtype)
    del _x0
    return _d

def reference(L0_attn_x, L0_attn_Wq, L0_attn_bq, L0_attn_Wk, L0_attn_bk, L0_attn_Wv, L0_attn_bv, L0_attn_Wo, L0_attn_bo, L0_ffn_gate_w, L0_ffn_up_w, L0_ffn_down_w, L0_ffn_gate_s, L0_ffn_up_s, L0_ffn_down_s):

    def _L0_attn_ref(x, Wq, bq, Wk, bk, Wv, bv, Wo, bo):
        import jax, jax.numpy as jnp
        import numpy as np
        HEAD_NUM = 16
        ROPE_BASE = 10000.0

        def _rotate_half(x):
            x_even = x[..., ::2]
            x_odd = x[..., 1::2]
            return jnp.stack((-x_odd, x_even), axis=-1).reshape(x.shape)

        def _rope_cos_sin(seq_len, head_dim):
            half = head_dim // 2
            inv_freq = 1.0 / ROPE_BASE ** (jnp.arange(half, dtype=jnp.float32) / half)
            t = jnp.arange(seq_len, dtype=jnp.float32)
            freqs = t[:, None] * inv_freq[None, :]
            cos = jnp.repeat(jnp.cos(freqs), 2, axis=-1)
            sin = jnp.repeat(jnp.sin(freqs), 2, axis=-1)
            return (cos, sin)
        B, S, H = x.shape
        nh = HEAD_NUM
        d = H // nh
        scale = jnp.float32(np.sqrt(d))

        def proj(W, b):
            y = x @ W.T + b
            return y.reshape(B, S, nh, d).transpose(0, 2, 1, 3)
        Q = proj(Wq, bq)
        K = proj(Wk, bk)
        V = proj(Wv, bv)
        cos, sin = _rope_cos_sin(S, d)
        Q = Q * cos + _rotate_half(Q) * sin
        K = K * cos + _rotate_half(K) * sin
        scores = jnp.einsum('bhqd,bhkd->bhqk', Q, K) / scale
        causal = jnp.tril(jnp.ones((S, S), dtype=bool))
        scores = jnp.where(causal, scores, jnp.float32(-jnp.inf))
        attn = jax.nn.softmax(scores, axis=-1)
        out = jnp.einsum('bhqk,bhkd->bhqd', attn, V)
        out = out.transpose(0, 2, 1, 3).reshape(B, S, H)
        return out @ Wo.T + bo

    def _L0_ffn_ref(x, gate_w, up_w, down_w, gate_s, up_s, down_s):
        import jax, jax.numpy as jnp
        import numpy as np
        HIDDEN = 512
        INTER = 1408
        B, S = (2, 512)

        def _ternary(key, shape):
            return jax.random.randint(key, shape, -1, 2).astype(jnp.float32)
        b, s, h = x.shape
        xf = x.reshape(b * s, h)
        g = jnp.einsum('th,ih->ti', xf, gate_w) * gate_s
        u = jnp.einsum('th,ih->ti', xf, up_w) * up_s
        hdn = jax.nn.silu(g) * u
        out = jnp.einsum('ti,hi->th', hdn, down_w) * down_s
        return out.reshape(b, s, -1)
    x = L0_attn_x
    x = x + _L0_attn_ref(_layernorm(x, axis=-1), L0_attn_Wq, L0_attn_bq, L0_attn_Wk, L0_attn_bk, L0_attn_Wv, L0_attn_bv, L0_attn_Wo, L0_attn_bo)
    x = x + _L0_ffn_ref(_layernorm(x, axis=-1), L0_ffn_gate_w, L0_ffn_up_w, L0_ffn_down_w, L0_ffn_gate_s, L0_ffn_up_s, L0_ffn_down_s)
    return x

_drawn_inputs = setup_inputs


def setup_inputs(seed=0):
    import zlib

    import numpy as np

    out = dict(_drawn_inputs(seed))
    spreads = {}
    factors = {'L0_attn_bq': 8.0, 'L0_attn_bk': 8.0}
    for name, (base, spread) in spreads.items():
        noise = np.random.default_rng([zlib.crc32(name.encode()), seed]).standard_normal(out[name].shape)
        drawn = base * np.exp(spread * noise) if base else spread * noise
        out[name] = jnp.asarray(drawn.astype(out[name].dtype))
    for name, factor in factors.items():
        out[name] = (out[name] * factor).astype(out[name].dtype)
    return out
```

```python
from contextlib import ExitStack

import concourse.bass as bass
from concourse import mybir

ALU = mybir.AluOpType
ACT = mybir.ActivationFunctionType
AX_X = mybir.AxisListType.X
F32 = mybir.dt.float32
F32R = mybir.dt.float32r
F16 = mybir.dt.float16
BF16 = mybir.dt.bfloat16
I32 = mybir.dt.int32

P = 128
NB, S, H = 2, 1024, 512
NH, D = 16, 32
INTER = 1408
KC = H // P
IT = INTER // P
CH = 512
CC = S // CH
TJ = CH // P
KT = S // P
HEADS = NB * NH
HALF = P // (D // 2)
VW = 3 * D + 1
VP = VW + 1
SCALE = float(1.0 / (D ** 0.5))
LN_EPS = 1e-5
NEG = -1e30
P_SHIFT = 14 * 0.6931471805599453
SLOTS = 4
K_DOT = 3 * D
K_ALL = K_DOT + 2

S_PIECES = []
for qt in range(KT):
    need = P * (qt + 1)
    if need <= 512:
        S_PIECES.append((qt, 0, max(need, 256), 0))
    else:
        first = 384 if need == 640 else 512
        S_PIECES += [(qt, 0, first, 0), (qt, first, need - first, 1)]
ST_PIECES = [(0, 0, 512, 0), (0, 512, 512, 512), (1, 128, 384, 128), (1, 512, 512, 512),
             (2, 256, 384, 256), (2, 640, 384, 640), (3, 384, 384, 384), (3, 768, 256, 768),
             (4, 512, 512, 512), (5, 640, 384, 640), (6, 768, 256, 768), (7, 768, 256, 896)]
NPC = len(S_PIECES)
assert NPC == len(ST_PIECES) == 12
LAST_PIECE = [max(i for i, p in enumerate(ST_PIECES) if p[0] == kt) for kt in range(KT)]
P_OFF = [sum(S - P * k for k in range(kt)) for kt in range(KT + 1)]
POOL_KT = 5
DVE_KT = KT - POOL_KT
FFN_COLS = KC * INTER
W_PIECE = 2 * H
FLAG_W = 704
FLAG_N = 3 * FFN_COLS // FLAG_W
assert IT * H == FFN_COLS


def transformer_block(nc, x, wq, wk, wv, wo, bqk, bv, bo, ffn, gs, us, ds, cos, sin, out):
    ctx = ExitStack()
    with ctx:
        def sb(name, shape, dt, scope=ctx):
            return scope.enter_context(nc.sbuf_tensor(name, shape, dt))

        def sem(name):
            return ctx.enter_context(nc.semaphore(name))

        scratch = nc.dram_tensor("qk_scratch", [2, 4, HEADS, D // 2, S], F32, kind="Internal").ap()
        ffn_copy = nc.dram_tensor("ffn_copy", [P, 3 * FFN_COLS], F32, kind="Internal").ap()

        xT_hi = sb("xT_hi", [P, KC, CH], F32R)
        xT_lo = sb("xT_lo", [P, KC, CH], F32R)
        ident = sb("ident", [P, P], F32)
        ident_b = sb("ident_b", [P, P], BF16)
        mask_kq = sb("mask_kq", [P, P], BF16)
        mask_qk = sb("mask_qk", [P, P], BF16)
        stats = sb("stats", [P, TJ, 6], F32)
        moments = sb("moments", [P, TJ, 2], F32)
        std = sb("std", [P, TJ], F32)
        rstd = sb("rstd", [P, TJ], F32)
        eps = sb("eps", [P, 1], F32)
        shift = sb("shift", [P, 1], F32)
        bqk_sb = sb("bqk_sb", [P, 8], F32)
        gs_sb = sb("gs_sb", [P, IT], F32)
        us_sb = sb("us_sb", [P, IT], F32)
        flag_max = sb("flag_max", [P, FLAG_N], I32)
        flag_part = sb("flag_part", [P, 1], F32)
        flag_all = sb("flag_all", [P, 1], F32)
        flag_int = sb("flag_int", [P, 1], I32)
        with ExitStack() as under_tok:
            rot = sb("rot", [P, 2, 2, CH], F32, under_tok)
            st_hi = sb("st_hi", [P, 2, 2, CH], F32R, under_tok)
            st_lo = sb("st_lo", [P, 2, 2, CH], F32R, under_tok)
            even = sb("even", [P, 2, CH], F32, under_tok)
            odd = sb("odd", [P, 2, CH], F32, under_tok)
        tok = sb("tok", [P, KT, NB, H], F32)
        with ExitStack() as stage_ab:
            v_sb = sb("v_sb", [P, KT, HEADS, VP], BF16, stage_ab)
            with ExitStack() as stage_a:
                w_hi = [sb(f"w_hi{m}", [P, KC, H], F32R, stage_a) for m in range(3)]
                w_lo = [sb(f"w_lo{m}", [P, KC, H], F32R, stage_a) for m in range(3)]
                w_st = sb("w_st", [P, 2, W_PIECE], F32, stage_a)
                xst_a = sb("xst_a", [P, CC, TJ, H], F32, stage_a)
                cos_sb = sb("cos_sb", [P, S], F32, stage_a)
                sin_sb = sb("sin_sb", [P, S], F32, stage_a)
                bv_sb = sb("bv_sb", [P, H], F32, stage_a)
                ecos = sb("ecos", [P, CH], F32, stage_a)
                osin = sb("osin", [P, CH], F32, stage_a)
                ocos = sb("ocos", [P, 2, CH], F32, stage_a)
                esin = sb("esin", [P, 2, CH], F32, stage_a)
                v32 = sb("v32", [P, 2, H], F32, stage_a)
                v_rest = sb("v_rest", [P, 2, H], F32, stage_a)
            with ExitStack() as stage_b:
                q_st = sb("q_st", [P, SLOTS, S], F32R, stage_b)
                k_st = sb("k_st", [P, SLOTS, S], F32R, stage_b)
                p32 = sb("p32", [P, P_OFF[KT]], F32, stage_b)
                p_hi = sb("p_hi", [P, 2, P_OFF[KT]], F16, stage_b)
                p_lo = sb("p_lo", [P, 2, P_OFF[KT]], F16, stage_b)
                row_max = sb("row_max", [P, KT, 2], F32, stage_b)
                max8 = sb("max8", [P, KT], F32, stage_b)
                neg_max = sb("neg_max", [P, 2 * KT], F32R, stage_b)
                neg_max_T = sb("neg_max_T", [2 * KT, 2, P], F32, stage_b)
                o_sum = sb("o_sum", [P, KT, D], F32, stage_b)
                o_rec = sb("o_rec", [P, KT], F32, stage_b)
        wg_sb = sb("wg_sb", [P, KC, INTER], F32R)
        wu_sb = sb("wu_sb", [P, KC, INTER], F32R)
        wd_sb = sb("wd_sb", [P, IT, H], F32R)
        xh = sb("xh", [P, KT, NB, H], F32)
        xst_c = sb("xst_c", [P, TJ, H], F32)
        ds_sb = sb("ds_sb", [P, H], F32)
        with ExitStack() as stage_c1:
            wo_hi = sb("wo_hi", [P, KC, H], F32R, stage_c1)
            wo_lo = sb("wo_lo", [P, KC, H], F32R, stage_c1)
            xr = sb("xr", [P, CC, TJ, H], F32, stage_c1)
            bo_sb = sb("bo_sb", [P, H], F32, stage_c1)
        with ExitStack() as stage_c2:
            silu = sb("silu", [P, 2, CH], F32, stage_c2)
            hid = sb("hid", [P, 2, CH], F32, stage_c2)
            hid_hi = sb("hid_hi", [P, 3, CH], F32R, stage_c2)
            hid_lo = sb("hid_lo", [P, 3, CH], F32R, stage_c2)
            y_sb = sb("y_sb", [P, TJ, H], F32, stage_c2)
        wo_st = xh[:, 0:KT // 2, 0, :]

        ps = ctx.enter_context(nc.psum_tensor("ps", [P, 8, 512], F32))
        T_BANK, MM_BANK = 0, 4
        S_BANK, ST_BANK, O_BANK, M_BANK = 0, 2, 5, 7

        x_in = [sem(f"x_in{g}") for g in range(NB * CC)]
        const_in = sem("const_in")
        w_in = [sem(f"w_in{k}") for k in range(2)]
        ffn_copied = sem("ffn_copied")
        consts = sem("consts")
        w_hi_done = sem("w_hi_done")
        w_lo_done = sem("w_lo_done")
        low_bits = sem("low_bits")
        flag_done = sem("flag_done")
        ln_stats = sem("ln_stats")
        ln_moments = sem("ln_moments")
        ln_std = sem("ln_std")
        ln_rstd = sem("ln_rstd")
        ln_done = sem("ln_done")
        tokens_ready = sem("tokens_ready")
        t_ps = sem("t_ps")
        t_hi = sem("t_hi")
        t_lo = sem("t_lo")
        qk_ps = sem("qk_ps")
        eo_ready = sem("eo_ready")
        rope_prod = sem("rope_prod")
        pool_prod = sem("pool_prod")
        rope_done = sem("rope_done")
        rot_hi = sem("rot_hi")
        rot_lo = sem("rot_lo")
        scr_out = [sem(f"scr_out{k}") for k in range(2)]
        v_ps = sem("v_ps")
        v32_ready = sem("v32_ready")
        v1_ready = sem("v1_ready")
        rest_ready = sem("rest_ready")
        v2_ready = sem("v2_ready")
        v3_ready = sem("v3_ready")
        b_init = sem("b_init")
        row_max_init = sem("row_max_init")
        head_in = [sem(f"head_in{k}") for k in range(SLOTS)]
        s_ps = sem("s_ps")
        s_max = sem("s_max")
        max_step = sem("max_step")
        max_ready = sem("max_ready")
        max_T_ps = sem("max_T_ps")
        max_T = sem("max_T")
        max_in = [sem(f"max_in{k}") for k in range(SLOTS)]
        st_ps = sem("st_ps")
        exp_done = sem("exp_done")
        p_hi_done = sem("p_hi_done")
        p_lo_pool = sem("p_lo_pool")
        p_lo_dve = sem("p_lo_dve")
        pv_done = sem("pv_done")
        o_parts = sem("o_parts")
        o_done = sem("o_done")
        wo_in = sem("wo_in")
        wo_hi_done = sem("wo_hi_done")
        wo_lo_done = sem("wo_lo_done")
        c_in = sem("c_in")
        ffn_in = sem("ffn_in")
        xr_in = [sem(f"xr_in{k}") for k in range(NB * CC)]
        xr_ready = sem("xr_ready")
        o_ps = sem("o_ps")
        x2_ready = sem("x2_ready")
        flag_ready = sem("flag_ready")
        g_ps = sem("g_ps")
        u_ps = sem("u_ps")
        silu_ready = sem("silu_ready")
        hid_ready = sem("hid_ready")
        hid_hi_done = sem("hid_hi_done")
        hid_lo_done = sem("hid_lo_done")
        down_ps = sem("down_ps")
        y_scaled = sem("y_scaled")
        y_ready = sem("y_ready")
        y_out = [sem(f"y_out{j}") for j in range(TJ)]

        N_CH = NB * CC
        block = ctx.enter_context(nc.Block())

        def stage_a_done(eng):
            eng.wait_ge(v32_ready, N_CH * TJ)
            eng.wait_ge(v2_ready, N_CH * TJ)
            eng.wait_ge(v3_ready, N_CH * TJ)
            eng.wait_ge(v_ps, N_CH * TJ)
            for k in range(2):
                eng.wait_ge(scr_out[k], 64 * 2 * N_CH)

        def stage_b_done(eng):
            eng.wait_ge(pv_done, HEADS)
            eng.wait_ge(o_done, HEADS)
            eng.wait_ge(st_ps, NPC * HEADS)
            eng.wait_ge(s_max, NPC * HEADS)
            eng.wait_ge(max_T, HEADS)

        def stage_c1_done(eng):
            eng.wait_ge(o_ps, N_CH * TJ)
            eng.wait_ge(x2_ready, N_CH * TJ)

        def chunks(eng):
            with eng.Fori(0, NB) as b:
                for cc in range(CC):
                    yield b, cc, b * CC + cc

        def steps():
            return range(0, SLOTS), range(SLOTS), range(HEADS - SLOTS, HEADS + 1)

        @block.sync
        def _(sp):
            def load_x(dst, b, cc):
                return sp.dma_start(dst[:, cc, :, :], x[b, cc * CH:(cc + 1) * CH, :].rearrange("(j p) h -> p j h", p=P))

            load_x(xst_a, 0, 0).then_inc(x_in[0], 16)
            sp.dma_start(bqk_sb[:, :], bqk).then_inc(const_in, 16)
            sp.dma_start(cos_sb[:, :], cos).then_inc(const_in, 16)
            sp.dma_start(sin_sb[:, :], sin).then_inc(const_in, 16)
            sp.dma_start(bv_sb[:, :], bv.partition_broadcast(P)).then_inc(const_in, 16)
            sp.dma_start(gs_sb[:, :], gs).then_inc(const_in, 16)
            sp.dma_start(us_sb[:, :], us).then_inc(const_in, 16)
            for n in range(6):
                if n >= 2:
                    sp.wait_ge(w_lo_done, n - 1)
                src = (wq, wk, wv)[n // 2][:, n % 2 * W_PIECE:(n % 2 + 1) * W_PIECE]
                sp.dma_start(w_st[:, n % 2, :], src).then_inc(w_in[n % 2], 16)
                if n == 2:
                    load_x(xst_a, 0, 1).then_inc(x_in[1], 16)
            sp.dma_start(ffn_copy, ffn).then_inc(ffn_copied, 16)
            sp.wait_ge(w_lo_done, 6)

            def load_flag_piece(c, k):
                sp.wait_ge(flag_done, 6 * c + max(k - 1, 0))
                sp.dma_start(w_st[:, k % 2, 0:FLAG_W], ffn[:, bass.ds((6 * c + k) * FLAG_W, FLAG_W)]).then_inc(w_in[k % 2], 16)

            for b, cc, c in chunks(sp):
                load_flag_piece(c, 0)
                load_flag_piece(c, 1)
                for p in range(4):
                    for half, done, st in ((0, rot_hi, st_hi), (1, rot_lo, st_lo)):
                        sp.wait_ge(done, 4 * c + p + 1)
                        for eo in range(2):
                            dst = scratch[p // 2, 2 * half + eo, bass.ds(b * NH + p % 2 * HALF, HALF), :, cc * CH:(cc + 1) * CH]
                            sp.dma_start(dst.rearrange("h i s -> (h i) s"), st[:, p % 2, eo, :].bitcast(F32)).then_inc(scr_out[p % 2], 16)
                    load_flag_piece(c, p + 2)

            stage_a_done(sp)

            def load_head(t, slot):
                q, k = scratch[0], scratch[1]
                at = bass.ds(t, 1)
                hi, both = slice(0, 2), slice(0, 4)
                for dst, rows, src, parts in ((q_st, slice(0, 32), q, hi), (q_st, slice(32, 96), q, both),
                                              (k_st, slice(0, 64), k, both), (k_st, slice(64, 96), k, hi)):
                    sp.dma_start(dst[rows, slot, :].bitcast(F32), src[parts, at, :, :].rearrange("r o i s -> r (o i) s")).then_inc(head_in[slot], 16)

            def load_max(u, slot):
                sp.wait_ge(max_T, u + 1)
                for part in range(2):
                    sp.dma_start(q_st[K_DOT + part:K_DOT + part + 1, slot, :].bitcast(F32), neg_max_T[part * KT:(part + 1) * KT, slot % 2, :]).then_inc(max_in[slot], 16)

            def b_step(t, j, first=False, last=False):
                if not (last and j >= SLOTS - 1):
                    load_max(t + 1, (j + 1) % SLOTS)
                if not last:
                    sp.wait_ge(st_ps, NPC * (t + 1))
                    load_head(t + SLOTS, j)

            for t in range(SLOTS):
                load_head(t, t)
            load_max(0, 0)
            for t in range(SLOTS):
                b_step(t, t)
            with sp.Fori(1, HEADS // SLOTS - 1) as it:
                for j in range(SLOTS):
                    b_step(it * SLOTS + j, j)
            for j in range(SLOTS):
                b_step(HEADS - SLOTS + j, j, last=True)

            stage_b_done(sp)
            sp.dma_start(wo_st, wo).then_inc(wo_in, 16)
            sp.dma_start(bo_sb[:, :], bo.partition_broadcast(P)).then_inc(c_in, 16)
            sp.dma_start(ds_sb[:, :], ds.partition_broadcast(P)).then_inc(c_in, 16)
            load_x(xr, 0, 0).then_inc(xr_in[0], 16)
            load_x(xr, 0, 1).then_inc(xr_in[1], 16)
            sp.wait_ge(ffn_copied, 16)
            for m, dst in enumerate((wg_sb, wu_sb, wd_sb)):
                sp.dma_start(dst[:, :, :].rearrange("p a n -> p (a n)").bitcast(F32), ffn_copy[:, m * FFN_COLS:(m + 1) * FFN_COLS]).then_inc(ffn_in, 16)
            for cc in range(CC):
                sp.wait_ge(x2_ready, TJ * (cc + 1))
                load_x(xr, 1, cc).then_inc(xr_in[CC + cc], 16)
            for b, cc, c in chunks(sp):
                for j in range(TJ):
                    sp.wait_ge(y_ready, TJ * c + j + 1)
                    sp.dma_start(out[bass.ds(b, 1), cc * CH + j * P:cc * CH + (j + 1) * P, :].rearrange("o p h -> (o p) h"), y_sb[:, j, :]).then_inc(y_out[j], 16)
            for j in range(TJ):
                sp.wait_ge(y_out[j], 16 * N_CH)

        @block.gpsimd
        def _(pool):
            pool.memset(ident[:, :], 0.0)
            pool.memset(ident_b[:, :], 0.0)
            pool.memset(mask_kq[:, :], 0.0)
            pool.memset(mask_qk[:, :], 0.0)
            pool.memset(eps[:, :], LN_EPS)
            pool.memset(shift[:, :], P_SHIFT)
            pool.memset(v_sb[:, :, :, 3 * D:VP], 1.0).then_inc(consts, 1)
            pool.wait_ge(consts, 1)
            for m in (ident, ident_b):
                pool.affine_select(out=m[:, :], in_=m[:, :], compare_op=ALU.not_equal, fill=1.0, base=0,
                                   pattern=[[-1, P]], channel_multiplier=1)
            pool.affine_select(out=mask_kq[:, :], in_=mask_kq[:, :], compare_op=ALU.is_ge, fill=NEG, base=0,
                               pattern=[[1, P]], channel_multiplier=-1)
            pool.affine_select(out=mask_qk[:, :], in_=mask_qk[:, :], compare_op=ALU.is_ge, fill=NEG, base=0,
                               pattern=[[-1, P]], channel_multiplier=1).then_inc(consts, 1)
            pool.wait_ge(const_in, 96)

            for b, cc, c in chunks(pool):
                pos = slice(cc * CH, (cc + 1) * CH)
                for p in range(4):
                    n = 4 * c + p
                    pool.wait_ge(eo_ready, n + 1)
                    pool.wait_ge(rope_done, 4 * c + max(p - 1, 0))
                    pool.tensor_tensor(ocos[:, p % 2, :], odd[:, p % 2, :], cos_sb[:, pos], ALU.mult)
                    pool.tensor_tensor(esin[:, p % 2, :], even[:, p % 2, :], sin_sb[:, pos], ALU.mult).then_inc(pool_prod, 1)

                def rest(j):
                    pool.wait_ge(v1_ready, TJ * c + j + 1)
                    pool.wait_ge(v2_ready, TJ * c + max(j - 1, 0))
                    pool.wait_ge(v3_ready, TJ * c + max(j - 1, 0))
                    v1 = v_sb[:, cc * TJ + j, bass.ds(b * NH, NH), 0:D]
                    pool.tensor_tensor(v_rest[:, j % 2, :].rearrange("p (h d) -> p h d", d=D),
                                       v32[:, j % 2, :].rearrange("p (h d) -> p h d", d=D), v1, ALU.subtract).then_inc(rest_ready, 1)

                def third(j):
                    pool.wait_ge(v2_ready, TJ * c + j + 1)
                    v2 = v_sb[:, cc * TJ + j, bass.ds(b * NH, NH), D:2 * D]
                    v3 = v_sb[:, cc * TJ + j, bass.ds(b * NH, NH), 2 * D:3 * D]
                    pool.tensor_tensor(v3, v_rest[:, j % 2, :].rearrange("p (h d) -> p h d", d=D), v2, ALU.subtract).then_inc(v3_ready, 1)

                rest(0)
                rest(1)
                third(0)
                rest(2)
                third(1)
                rest(3)
                third(2)
                third(3)

            stage_a_done(pool)
            pool.memset(k_st[K_DOT:P, :, :].bitcast(F32), 1.0).then_inc(b_init, 1)
            pool.wait_ge(b_init, 1)

            def b_step(t, j):
                for kt in range(POOL_KT):
                    pool.wait_ge(p_hi_done, KT * t + kt + 1)
                    cols = slice(P_OFF[kt], P_OFF[kt + 1])
                    pool.tensor_tensor(p_lo[:, j % 2, cols], p32[:, cols], p_hi[:, j % 2, cols], ALU.subtract).then_inc(p_lo_pool, 1)

            with pool.Fori(0, HEADS // SLOTS) as it:
                for j in range(SLOTS):
                    b_step(it * SLOTS + j, j)

            stage_b_done(pool)
            pool.wait_ge(c_in, 32)
            for c in range(N_CH):
                pool.wait_ge(xr_in[c], 16)
                for j in range(TJ):
                    xt = xr[:, c % CC, j, :]
                    pool.tensor_tensor(xt, xt, bo_sb[:, :], ALU.add).then_inc(xr_ready, 1)
                if c == 0:
                    pool.wait_ge(flag_done, FLAG_N + 1)
                    pool.partition_all_reduce(flag_all[:, :], flag_part[:, :], P, bass.bass_isa.ReduceOp.max).then_inc(flag_ready, 1)
                    pool.wait_ge(flag_ready, 1)
                    pool.tensor_copy(flag_int[:, :], flag_all[:, :]).then_inc(flag_ready, 1)

            stage_c1_done(pool)
            for b, cc, c in chunks(pool):
                for i in range(IT):
                    pool.wait_ge(hid_hi_done, IT * c + i + 1)
                    pool.wait_ge(down_ps, IT * c + max(i - 2, 0))
                    pool.tensor_tensor(hid_lo[:, i % 3, :], hid[:, i % 2, :], hid_hi[:, i % 3, :].bitcast(F32), ALU.subtract).then_inc(hid_lo_done, 1)
                for j in range(TJ):
                    pool.wait_ge(y_scaled, TJ * c + j + 1)
                    pool.tensor_tensor(y_sb[:, j, :], y_sb[:, j, :], tok[:, cc * TJ + j, bass.ds(b, 1), :].rearrange("p o h -> p (o h)"), ALU.add).then_inc(y_ready, 1)

        @block.scalar
        def _(act):
            def std_of(n):
                act.wait_ge(ln_moments, n + 1)
                act.activation(std[:, :], moments[:, :, 1], ACT.Sqrt, bias=eps[:, 0:1]).then_inc(ln_std, 1)

            def transposed_hi(n):
                for kc in range(KC):
                    act.wait_ge(t_ps, KC * n + kc + 1)
                    act.copy(xT_hi[:, kc, :], ps[:, T_BANK + kc, :]).then_inc(t_hi, 1)

            act.wait_ge(consts, 2)
            std_of(0)
            for n in range(6):
                m, cols = n // 2, slice(n % 2 * 2, n % 2 * 2 + 2)
                act.wait_ge(w_in[n % 2], 16 * (n // 2 + 1))
                act.copy(w_hi[m][:, cols, :].rearrange("p a n -> p (a n)"), w_st[:, n % 2, :]).then_inc(w_hi_done, 1)
            act.wait_ge(const_in, 96)
            for c in range(N_CH):
                b, cc = divmod(c, CC)
                transposed_hi(c)
                if c + CC < N_CH:
                    act.dma_start(xst_a[:, cc, :, :], x[b + 1, cc * CH:(cc + 1) * CH, :].rearrange("(j p) h -> p j h", p=P)).then_inc(x_in[c + CC], 16)

                def evacuate(p):
                    n = 4 * c + p
                    act.wait_ge(qk_ps, n + 1)
                    if n >= 2:
                        act.wait_ge(rope_done, n - 1)
                    bank = MM_BANK + 2 * (p % 2)
                    act.activation(even[:, p % 2, :], ps[:, bank, :], ACT.Identity, bias=bqk_sb[:, 2 * p:2 * p + 1])
                    act.activation(odd[:, p % 2, :], ps[:, bank + 1, :], ACT.Identity, bias=bqk_sb[:, 2 * p + 1:2 * p + 2]).then_inc(eo_ready, 1)

                def high(p):
                    n = 4 * c + p
                    act.wait_ge(rope_done, n + 1)
                    if n >= 2:
                        act.wait_ge(scr_out[p % 2], 64 * (n // 2))
                    act.copy(st_hi[:, p % 2, :, :].rearrange("p e s -> p (e s)"),
                             rot[:, p % 2, :, :].rearrange("p e s -> p (e s)")).then_inc(rot_hi, 1)

                evacuate(0)
                evacuate(1)
                high(0)
                evacuate(2)
                high(1)
                evacuate(3)
                high(2)
                high(3)
                if c + 1 < N_CH:
                    std_of(c + 1)

                def v_part(j, part, src, ready, done):
                    act.wait_ge(ready, TJ * c + j + 1)
                    act.copy(v_sb[:, cc * TJ + j, b * NH:(b + 1) * NH, part * D:(part + 1) * D],
                             src[:, j % 2, :].rearrange("p (h d) -> p h d", d=D)).then_inc(done, 1)

                for j, part in ((0, 0), (1, 0), (0, 1), (2, 0), (1, 1), (3, 0), (2, 1), (3, 1)):
                    if part == 0:
                        v_part(j, 0, v32, v32_ready, v1_ready)
                    else:
                        v_part(j, 1, v_rest, rest_ready, v2_ready)

            stage_a_done(act)

            def exp_piece(t, j, i):
                kt, q0, w, keep = ST_PIECES[i]
                act.wait_ge(st_ps, NPC * t + i + 1)
                at = P_OFF[kt] + keep - P * kt
                act.activation(p32[:, at:at + q0 + w - keep], ps[:, ST_BANK + i % 3, keep - q0:w], ACT.Exp,
                               bias=shift[:, 0:1], scale=SCALE).then_inc(exp_done, 1)

            def b_step(t, j, it, first=False, last=False):
                def exps(kt):
                    if not (first and j == 0):
                        if kt < POOL_KT:
                            act.wait_ge(p_lo_pool, POOL_KT * (t - 1) + kt + 1)
                        else:
                            act.wait_ge(p_lo_dve, DVE_KT * (t - 1) + kt - POOL_KT + 1)
                    for i in range(NPC):
                        if ST_PIECES[i][0] == kt:
                            exp_piece(t, j, i)

                def high(kt):
                    act.wait_ge(exp_done, NPC * t + LAST_PIECE[kt] + 1)
                    cols = slice(P_OFF[kt], P_OFF[kt + 1])
                    act.copy(p_hi[:, j % 2, cols], p32[:, cols]).then_inc(p_hi_done, 1)

                if not (first and j < 2):
                    act.wait_ge(pv_done, t - 1)
                exps(0)
                exps(1)
                high(0)
                exps(2)
                high(1)
                exps(3)
                high(2)
                if not (last and j == SLOTS - 1):
                    act.wait_ge(max_T_ps, t + 2)
                    if not (first and j < 1):
                        act.wait_ge(max_in[(j - 1) % SLOTS], 32 * (it + (j - 1) // SLOTS + 1))
                    act.copy(neg_max_T[:, (j + 1) % 2, :], ps[0:2 * KT, M_BANK, 0:P]).then_inc(max_T, 1)
                for kt in range(4, KT):
                    exps(kt)
                    high(kt - 1)
                high(KT - 1)

            act.wait_ge(max_T_ps, 1)
            act.copy(neg_max_T[:, 0, :], ps[0:2 * KT, M_BANK, 0:P]).then_inc(max_T, 1)
            for j in range(SLOTS):
                b_step(j, j, 0, first=True)
            with act.Fori(1, HEADS // SLOTS - 1) as it:
                for j in range(SLOTS):
                    b_step(it * SLOTS + j, j, it)
            for j in range(SLOTS):
                b_step(HEADS - SLOTS + j, j, HEADS // SLOTS - 1, last=True)

            stage_b_done(act)

            def copy_tiles(src, b, cc):
                for j in range(TJ):
                    ins = act.copy(xst_c[:, j, :], src[:, cc * TJ + j, b, :])
                ins.then_inc(tokens_ready, 1)

            copy_tiles(tok, 0, 0)
            act.wait_ge(wo_in, 16)
            act.copy(wo_hi[:, :, :], wo_st).then_inc(wo_hi_done, 1)
            for c in range(N_CH):
                transposed_hi(N_CH + c)
                if c + 1 < N_CH:
                    copy_tiles(tok, *divmod(c + 1, CC))
                std_of(N_CH + c)

            act.wait_ge(ln_done, N_CH + 1)
            copy_tiles(xh, 0, 0)
            stage_c1_done(act)
            for c in range(N_CH):
                transposed_hi(2 * N_CH + c)
                if c + 1 < N_CH:
                    act.wait_ge(ln_done, N_CH + c + 2)
                    copy_tiles(xh, *divmod(c + 1, CC))
                for i in range(IT + 1):
                    n = IT * c + i
                    if i < IT:
                        act.wait_ge(g_ps, n + 1)
                        act.wait_ge(hid_ready, IT * c + max(i - 1, 0))
                        act.activation(silu[:, i % 2, :], ps[:, T_BANK + 2 * (i % 2), :], ACT.Silu, scale=gs_sb[:, i:i + 1]).then_inc(silu_ready, 1)
                    if i > 0:
                        act.wait_ge(hid_ready, n)
                        act.wait_ge(down_ps, IT * c + max(i - 3, 0))
                        act.copy(hid_hi[:, (i - 1) % 3, :], hid[:, (i - 1) % 2, :]).then_inc(hid_hi_done, 1)

        @block.vector
        def _(dve):
            def ln_first(n, tiles):
                for j in range(TJ):
                    ins = dve.bn_stats(stats[:, j, :], tiles[j])
                ins.then_inc(ln_stats, 1)
                dve.wait_ge(ln_stats, n + 1)
                for j in range(TJ):
                    ins = dve.bn_aggr(moments[:, j, :], stats[:, j, :])
                ins.then_inc(ln_moments, 1)

            def ln_second(n, tiles, outs):
                dve.wait_ge(ln_std, n + 1)
                dve.reciprocal(rstd[:, :], std[:, :]).then_inc(ln_rstd, 1)
                dve.wait_ge(ln_rstd, n + 1)
                for j in range(TJ):
                    ins = dve.tensor_scalar(outs[j], tiles[j], moments[:, j, 0:1], rstd[:, j:j + 1], ALU.subtract, ALU.mult)
                ins.then_inc(ln_done, 1)

            def transposed_lo(n):
                for kc in range(KC):
                    dve.wait_ge(t_hi, KC * n + kc + 1)
                    dve.tensor_tensor(xT_lo[:, kc, :], ps[:, T_BANK + kc, :], xT_hi[:, kc, :].bitcast(F32), ALU.subtract).then_inc(t_lo, 1)

            def a_tiles(c):
                return [xst_a[:, c % CC, j, :] for j in range(TJ)]

            dve.wait_ge(x_in[0], 16)
            ln_first(0, a_tiles(0))
            ln_second(0, a_tiles(0), a_tiles(0))
            for n in range(6):
                m, cols = n // 2, slice(n % 2 * 2, n % 2 * 2 + 2)
                dve.wait_ge(w_hi_done, n + 1)
                dve.tensor_tensor(w_lo[m][:, cols, :].rearrange("p a n -> p (a n)"), w_st[:, n % 2, :],
                                  w_hi[m][:, cols, :].rearrange("p a n -> p (a n)").bitcast(F32), ALU.subtract).then_inc(w_lo_done, 1)
            dve.wait_ge(const_in, 96)
            for c in range(N_CH):
                cc = c % CC
                pos = slice(cc * CH, (cc + 1) * CH)
                transposed_lo(c)

                def rotate(p):
                    n = 4 * c + p
                    dve.wait_ge(eo_ready, n + 1)
                    if n >= 1:
                        dve.wait_ge(rope_done, n)
                    dve.tensor_tensor(ecos[:, :], even[:, p % 2, :], cos_sb[:, pos], ALU.mult)
                    dve.tensor_tensor(osin[:, :], odd[:, p % 2, :], sin_sb[:, pos], ALU.mult).then_inc(rope_prod, 1)
                    dve.wait_ge(rope_prod, n + 1)
                    if n >= 2:
                        dve.wait_ge(rot_hi, n - 1)
                    dve.tensor_tensor(rot[:, p % 2, 0, :], ecos[:, :], osin[:, :], ALU.subtract)
                    dve.wait_ge(pool_prod, n + 1)
                    dve.tensor_tensor(rot[:, p % 2, 1, :], ocos[:, p % 2, :], esin[:, p % 2, :], ALU.add).then_inc(rope_done, 1)

                def low(p):
                    n = 4 * c + p
                    dve.wait_ge(rot_hi, n + 1)
                    dve.tensor_tensor(st_lo[:, p % 2, :, :].rearrange("p e s -> p (e s)"), rot[:, p % 2, :, :].rearrange("p e s -> p (e s)"),
                                      st_hi[:, p % 2, :, :].rearrange("p e s -> p (e s)").bitcast(F32), ALU.subtract).then_inc(rot_lo, 1)

                def test_piece(k):
                    f = 6 * c + k
                    piece = w_st[:, k % 2, 0:FLAG_W].bitcast(I32)
                    dve.wait_ge(w_in[k % 2], 16 * (3 + f // 2 + 1))
                    dve.tensor_single_scalar(piece, piece, (1 << 12) - 1, ALU.bitwise_and).then_inc(low_bits, 1)
                    dve.wait_ge(low_bits, f + 1)
                    dve.tensor_reduce(flag_max[:, f:f + 1], piece, AX_X, ALU.max).then_inc(flag_done, 1)

                def v_bias(j):
                    idx = TJ * c + j
                    dve.wait_ge(v_ps, idx + 1)
                    if idx >= 2:
                        dve.wait_ge(rest_ready, idx - 1)
                    dve.tensor_tensor(v32[:, j % 2, :], ps[:, MM_BANK + j, :], bv_sb[:, :], ALU.add).then_inc(v32_ready, 1)

                rotate(0)
                rotate(1)
                low(0)
                test_piece(0)
                rotate(2)
                low(1)
                test_piece(1)
                rotate(3)
                low(2)
                test_piece(2)
                low(3)
                test_piece(3)
                if c + 1 < N_CH:
                    dve.wait_ge(x_in[c + 1], 16)
                    ln_first(c + 1, a_tiles(c + 1))
                v_bias(0)
                test_piece(4)
                v_bias(1)
                test_piece(5)
                if c + 1 < N_CH:
                    ln_second(c + 1, a_tiles(c + 1), a_tiles(c + 1))
                v_bias(2)
                v_bias(3)
            dve.wait_ge(flag_done, FLAG_N)
            dve.tensor_reduce(flag_part[:, :], flag_max[:, :], AX_X, ALU.max).then_inc(flag_done, 1)

            stage_a_done(dve)
            dve.memset(row_max[:, :, :], NEG).then_inc(row_max_init, 1)
            dve.wait_ge(row_max_init, 1)

            def max_piece(u, i):
                qt, k0, w, part = S_PIECES[i]
                dve.wait_ge(s_ps, NPC * u + i + 1)
                kept = min(w, P * (qt + 1) - k0)
                dve.tensor_reduce(row_max[:, qt, part:part + 1], ps[:, S_BANK + i % 2, 0:kept], AX_X, ALU.max).then_inc(s_max, 1)

            def negate_max(u):
                dve.wait_ge(s_max, NPC * (u + 1))
                dve.tensor_reduce(max8[:, :], row_max[:, :, :], AX_X, ALU.max).then_inc(max_step, 1)
                dve.wait_ge(max_step, 2 * u + 1)
                dve.wait_ge(max_T_ps, u)
                dve.tensor_scalar(neg_max[:, 0:KT], max8[:, :], -1.0, None, ALU.mult).then_inc(max_step, 1)
                dve.wait_ge(max_step, 2 * u + 2)
                dve.scalar_tensor_tensor(out=neg_max[:, KT:2 * KT], in0=max8[:, :], scalar=-1.0, in1=neg_max[:, 0:KT].bitcast(F32),
                                         op0=ALU.mult, op1=ALU.subtract).then_inc(max_ready, 1)

            def b_step(t, j, first=False, tail=None):
                scores = tail is None or tail + 2 < HEADS
                before = not (first and j == 0)
                if scores:
                    for i in range(3):
                        max_piece(t + 2, i)
                if before:
                    r, half = t - 1, (j - 1) % 2
                    for kt in range(POOL_KT, KT):
                        dve.wait_ge(p_hi_done, KT * r + kt + 1)
                        cols = slice(P_OFF[kt], P_OFF[kt + 1])
                        dve.tensor_tensor(p_lo[:, half, cols], p32[:, cols], p_hi[:, half, cols], ALU.subtract).then_inc(p_lo_dve, 1)
                if scores:
                    for i in range(3, NPC):
                        max_piece(t + 2, i)
                    negate_max(t + 2)
                if before:
                    dve.wait_ge(pv_done, t)
                    for g in range(2):
                        o = ps[:, O_BANK + g, 0:4 * VW].rearrange("p (q e) -> p q e", e=VW)
                        q4 = slice(4 * g, 4 * g + 4)
                        dve.tensor_reduce(o_sum[:, q4, :], o[:, :, 0:3 * D].rearrange("p q (s d) -> p q d s", d=D), AX_X, ALU.add)
                        ins = dve.reciprocal(o_rec[:, q4], o[:, :, 3 * D])
                    ins.then_inc(o_parts, 1)
                    dve.wait_ge(o_parts, t)
                    dst = tok[:, :, :, :].rearrange("p k b (h d) -> p k (b h) d", d=D)[:, :, bass.ds(r, 1), :].rearrange("p k o d -> p k (o d)")
                    dve.tensor_tensor(dst, o_sum[:, :, :], o_rec[:, :].unsqueeze(2).broadcast_to([P, KT, D]), ALU.mult).then_inc(o_done, 1)

            for u in range(2):
                for i in range(NPC):
                    max_piece(u, i)
                negate_max(u)
            for j in range(SLOTS):
                b_step(j, j, first=True)
            with dve.Fori(1, HEADS // SLOTS - 1) as it:
                for j in range(SLOTS):
                    b_step(it * SLOTS + j, j)
            for j in range(SLOTS + 1):
                b_step(HEADS - SLOTS + j, j % SLOTS, tail=HEADS - SLOTS + j)

            stage_b_done(dve)
            dve.wait_ge(wo_hi_done, 1)
            dve.tensor_tensor(wo_lo[:, :, :], wo_st, wo_hi[:, :, :].bitcast(F32), ALU.subtract).then_inc(wo_lo_done, 1)

            def c_tiles(src, c):
                b, cc = divmod(c, CC)
                return [src[:, cc * TJ + j, b, :] for j in range(TJ)]

            for c in range(N_CH):
                transposed_lo(N_CH + c)
                if c == 1:
                    dve.wait_ge(wo_lo_done, 1)
                if c > 0:
                    ln_second(N_CH + c - 1, c_tiles(tok, c - 1), c_tiles(xh, c - 1))
                for j, x2 in enumerate(c_tiles(tok, c)):
                    dve.wait_ge(o_ps, TJ * c + j + 1)
                    dve.wait_ge(xr_ready, TJ * c + j + 1)
                    dve.tensor_tensor(x2, ps[:, MM_BANK + j, :], xr[:, c % CC, j, :], ALU.add).then_inc(x2_ready, 1)
                dve.wait_ge(x2_ready, TJ * (c + 1))
                ln_first(N_CH + c, c_tiles(tok, c))
            ln_second(2 * N_CH - 1, c_tiles(tok, N_CH - 1), c_tiles(xh, N_CH - 1))

            stage_c1_done(dve)
            dve.wait_ge(c_in, 32)
            for b, cc, c in chunks(dve):
                transposed_lo(2 * N_CH + c)
                for i in range(IT):
                    n = IT * c + i
                    dve.wait_ge(u_ps, n + 1)
                    dve.wait_ge(silu_ready, n + 1)
                    dve.wait_ge(hid_lo_done, IT * c + max(i - 1, 0))
                    dve.scalar_tensor_tensor(out=hid[:, i % 2, :], in0=ps[:, T_BANK + 2 * (i % 2) + 1, :], scalar=us_sb[:, i:i + 1],
                                             in1=silu[:, i % 2, :], op0=ALU.mult, op1=ALU.mult).then_inc(hid_ready, 1)
                dve.wait_ge(down_ps, IT * (c + 1))
                for j in range(TJ):
                    dve.wait_ge(y_out[j], 16 * c)
                    dve.tensor_tensor(y_sb[:, j, :], ps[:, MM_BANK + j, :], ds_sb[:, :], ALU.mult).then_inc(y_scaled, 1)

        @block.tensor
        def _(pe):
            def transpose_chunk(n, tiles, ready, count):
                pe.wait_ge(ready, count)
                pe.wait_ge(t_lo, KC * n)
                for kc in range(KC):
                    for j in range(TJ):
                        ins = pe.transpose(ps[:, T_BANK + kc, j * P:(j + 1) * P], tiles[j][:, kc * P:(kc + 1) * P], ident[:, :])
                    ins.then_inc(t_ps, 1)

            def product(dst, terms):
                for k, (w, m) in enumerate(terms):
                    ins = pe.matmul(dst, w, m, start=(k == 0), stop=(k == len(terms) - 1))
                return ins

            pe.wait_ge(consts, 2)
            for b, cc, c in chunks(pe):
                transpose_chunk(c, [xst_a[:, cc, j, :] for j in range(TJ)], ln_done, c + 1)
                pe.wait_ge(v32_ready, TJ * c)
                pe.wait_ge(t_hi, KC * (c + 1))
                pe.wait_ge(t_lo, KC * (c + 1))
                for p in range(4):
                    pe.wait_ge(w_lo_done, 2 if p < 2 else 4)
                    if p >= 2:
                        pe.wait_ge(eo_ready, 4 * c + p - 1)
                    m, half = p // 2, p % 2
                    for eo in range(2):
                        cols = slice((2 * half + eo) * P, (2 * half + eo + 1) * P)
                        ins = product(ps[:, MM_BANK + 2 * half + eo, :],
                                      [(w[m][:, kc, cols], xT[:, kc, :]) for w, xT in ((w_hi, xT_hi), (w_lo, xT_hi), (w_hi, xT_lo)) for kc in range(KC)])
                    ins.then_inc(qk_ps, 1)
                pe.wait_ge(w_lo_done, 6)
                for j in range(TJ):
                    pe.wait_ge(eo_ready, 4 * c + 3 + j // 2)
                    tile = slice(j * P, (j + 1) * P)
                    product(ps[:, MM_BANK + j, :],
                            [(xT[:, kc, tile], w[2][:, kc, :]) for w, xT in ((w_hi, xT_hi), (w_lo, xT_hi), (w_hi, xT_lo)) for kc in range(KC)]).then_inc(v_ps, 1)

            pe.wait_ge(t_lo, KC * N_CH)
            pe.wait_ge(v32_ready, N_CH * TJ)
            pe.wait_ge(v3_ready, N_CH * TJ)
            pe.wait_ge(b_init, 1)

            def score_piece(u, slot, uses, i, first=False):
                qt, k0, w, _ = S_PIECES[i]
                if i == 0:
                    pe.wait_ge(head_in[slot], 64 * uses)
                if not (first and i < 2):
                    pe.wait_ge(s_max, NPC * u + i - 1)
                dst = ps[:, S_BANK + i % 2, :]
                diagonal = k0 + w > P * qt
                ins = pe.matmul(dst[:, 0:w], q_st[0:K_DOT, slot, qt * P:(qt + 1) * P], k_st[0:K_DOT, slot, k0:k0 + w],
                                start=True, stop=not diagonal)
                if diagonal:
                    d0 = P * qt - k0
                    ins = pe.matmul(dst[:, d0:d0 + P], ident_b[:, :], mask_qk[:, :], start=False, stop=True)
                ins.then_inc(s_ps, 1)

            def shifted_piece(t, slot, uses, i, first=False):
                kt, q0, w, keep = ST_PIECES[i]
                if i == 0:
                    pe.wait_ge(max_in[slot], 32 * uses)
                if not (first and i < 3):
                    pe.wait_ge(exp_done, NPC * t + i - 2)
                diagonal = i == 0 or ST_PIECES[i - 1][0] != kt
                dst = ps[:, ST_BANK + i % 3, :]
                ins = pe.matmul(dst[:, 0:w], k_st[0:K_ALL, slot, kt * P:(kt + 1) * P], q_st[0:K_ALL, slot, q0:q0 + w],
                                start=True, stop=not diagonal)
                if diagonal:
                    d0 = P * kt - q0
                    ins = pe.matmul(dst[:, d0:d0 + P], ident_b[:, :], mask_kq[:, :], start=False, stop=True)
                ins.then_inc(st_ps, 1)

            def transpose_max(u):
                pe.wait_ge(max_ready, u + 1)
                pe.wait_ge(max_T, u)
                pe.transpose(ps[0:2 * KT, M_BANK, 0:P], neg_max[:, :].bitcast(F32), ident[:, :]).then_inc(max_T_ps, 1)

            def pv_tile(r, half, kt):
                if kt == 0:
                    pe.wait_ge(o_done, r)
                pe.wait_ge(p_hi_done, KT * r + kt + 1)
                if kt < POOL_KT:
                    pe.wait_ge(p_lo_pool, POOL_KT * r + kt + 1)
                else:
                    pe.wait_ge(p_lo_dve, DVE_KT * r + kt - POOL_KT + 1)
                v = v_sb[:, kt, bass.ds(r, 1), 0:VW].rearrange("p o e -> p (o e)")
                for qt in range(kt, KT):
                    at = P_OFF[kt] + (qt - kt) * P
                    dst = ps[:, O_BANK + qt // 4, qt % 4 * VW:(qt % 4 + 1) * VW]
                    for k, part in enumerate((p_hi, p_lo)):
                        ins = pe.matmul(dst, part[:, half, at:at + P], v, start=(kt == 0 and qt % 4 == 0 and k == 0),
                                        stop=(kt == qt and k == 1), skip_group_check=True)
                if kt == KT - 1:
                    ins.then_inc(pv_done, 1)

            PV_AFTER = [0, 1, 3, 4, 6, 7, 9, 10]

            def b_step(t, j, it, first=False, tail=None):
                for i in range(NPC):
                    if tail is None or tail < HEADS:
                        shifted_piece(t, j, it + 1, i, first and j == 0)
                    if tail is None or tail + 2 < HEADS:
                        score_piece(t + 2, (j + 2) % SLOTS, it + (j + 2) // SLOTS + 1, i)
                    if i == 5 and (tail is None or tail + 1 < HEADS):
                        transpose_max(t + 1)
                    if i in PV_AFTER and not (first and j == 0):
                        pv_tile(t - 1, (j - 1) % 2, PV_AFTER.index(i))

            for u in range(2):
                for i in range(NPC):
                    score_piece(u, u, 1, i, first=(u == 0))
                if u == 0:
                    transpose_max(0)
            for j in range(SLOTS):
                b_step(j, j, 0, first=True)
            with pe.Fori(1, HEADS // SLOTS - 1) as it:
                for j in range(SLOTS):
                    b_step(it * SLOTS + j, j, it)
            for j in range(SLOTS + 1):
                b_step(HEADS - SLOTS + j, j % SLOTS, HEADS // SLOTS - 1, tail=HEADS - SLOTS + j)

            stage_b_done(pe)
            for b, cc, c in chunks(pe):
                transpose_chunk(c + N_CH, [xst_c[:, j, :] for j in range(TJ)], tokens_ready, c + 1)
                pe.wait_ge(x2_ready, TJ * c)
                pe.wait_ge(wo_lo_done, 1)
                pe.wait_ge(t_hi, KC * (c + N_CH + 1))
                pe.wait_ge(t_lo, KC * (c + N_CH + 1))
                for j in range(TJ):
                    tile = slice(j * P, (j + 1) * P)
                    product(ps[:, MM_BANK + j, :],
                            [(xT[:, kc, tile], w[:, kc, :]) for w, xT in ((wo_hi, xT_hi), (wo_lo, xT_hi), (wo_hi, xT_lo)) for kc in range(KC)]).then_inc(o_ps, 1)

            def ffn_products(dt):
                def t(ap):
                    return ap if dt == F32R else ap.bitcast(F32)

                pe.wait_ge(x2_ready, TJ * N_CH)
                pe.wait_ge(ffn_in, 48)
                for b, cc, c in chunks(pe):
                    pe.wait_ge(hid_ready, IT * c)
                    transpose_chunk(c + 2 * N_CH, [xst_c[:, j, :] for j in range(TJ)], tokens_ready, c + N_CH + 1)
                    pe.wait_ge(t_hi, KC * (c + 2 * N_CH + 1))
                    pe.wait_ge(t_lo, KC * (c + 2 * N_CH + 1))

                    def gate_up(i):
                        n = IT * c + i
                        if i >= 2:
                            pe.wait_ge(hid_ready, n - 1)
                        cols = slice(i * P, (i + 1) * P)
                        for k, (w, done) in enumerate(((wg_sb, g_ps), (wu_sb, u_ps))):
                            product(ps[:, T_BANK + 2 * (i % 2) + k, :],
                                    [(t(w[:, kc, cols]), t(xT[:, kc, :])) for kc in range(KC) for xT in (xT_hi, xT_lo)]).then_inc(done, 1)

                    def down(i):
                        if i == 0:
                            pe.wait_ge(y_scaled, TJ * c)
                        pe.wait_ge(hid_hi_done, IT * c + i + 1)
                        pe.wait_ge(hid_lo_done, IT * c + i + 1)
                        for j in range(TJ):
                            tile = slice(j * P, (j + 1) * P)
                            for k, h in enumerate((hid_hi, hid_lo)):
                                ins = pe.matmul(ps[:, MM_BANK + j, :], t(h[:, i % 3, tile]), t(wd_sb[:, i, :]),
                                                start=(i == 0 and k == 0), stop=(i == IT - 1 and k == 1))
                        ins.then_inc(down_ps, 1)

                    gate_up(0)
                    for i in range(1, IT):
                        gate_up(i)
                        down(i - 1)
                    down(IT - 1)

            pe.wait_ge(flag_ready, 2)
            inexact = pe.value_load(flag_int[0:1, 0:1])
            with pe.If(inexact == 0):
                ffn_products(F32R)
            with pe.Else():
                ffn_products(F32)


def kernel(L0_attn_x, L0_attn_Wq, L0_attn_bq, L0_attn_Wk, L0_attn_bk, L0_attn_Wv, L0_attn_bv, L0_attn_Wo, L0_attn_bo,
           L0_ffn_gate_w, L0_ffn_up_w, L0_ffn_down_w, L0_ffn_gate_s, L0_ffn_up_s, L0_ffn_down_s):
    import numpy as np
    import concourse.bacc as bacc
    from concourse.bass_utils import run_bass_kernel_spmd

    def rows_on_partitions(w):
        return np.ascontiguousarray(np.asarray(w).reshape(-1, P, w.shape[1]).transpose(1, 0, 2).reshape(P, -1))

    order = np.arange(H).reshape(2, HALF, D // 2, 2).transpose(0, 3, 1, 2).reshape(-1)

    def per_partition(v, n):
        return np.ascontiguousarray(np.asarray(v).reshape(n, P).T)

    inv_freq = (1.0 / np.float32(10000.0) ** (np.arange(D // 2, dtype=np.float32) / np.float32(D // 2))).astype(np.float32)
    freqs = np.arange(S, dtype=np.float32)[None, :] * inv_freq[:, None]
    wq, wk = np.asarray(L0_attn_Wq), np.asarray(L0_attn_Wk)
    arrays = {
        "x": np.ascontiguousarray(L0_attn_x),
        "wq": rows_on_partitions(wq[order].T), "wk": rows_on_partitions(wk[order].T),
        "wv": rows_on_partitions(np.asarray(L0_attn_Wv).T), "wo": rows_on_partitions(np.asarray(L0_attn_Wo).T),
        "bqk": np.concatenate([per_partition(np.asarray(v)[order], KC) for v in (L0_attn_bq, L0_attn_bk)], axis=1),
        "bv": np.ascontiguousarray(L0_attn_bv), "bo": np.ascontiguousarray(L0_attn_bo),
        "ffn": np.concatenate([rows_on_partitions(np.asarray(w).T) for w in (L0_ffn_gate_w, L0_ffn_up_w, L0_ffn_down_w)], axis=1),
        "gs": per_partition(L0_ffn_gate_s, IT), "us": per_partition(L0_ffn_up_s, IT), "ds": np.ascontiguousarray(L0_ffn_down_s),
        "cos": np.tile(np.cos(freqs).astype(np.float32), (HALF, 1)), "sin": np.tile(np.sin(freqs).astype(np.float32), (HALF, 1)),
    }
    nc = bacc.Bacc("TRN2", target_bir_lowering=False, num_devices=1)
    aps = {k: nc.dram_tensor(f"in_{k}", v.shape, mybir.dt.from_np(v.dtype), kind="ExternalInput").ap() for k, v in arrays.items()}
    out = nc.dram_tensor("out", (NB, S, H), F32, kind="ExternalOutput").ap()
    transformer_block(nc, out=out, **aps)
    r = run_bass_kernel_spmd(nc, [{f"in_{k}": v for k, v in arrays.items()}], core_ids=[0])
    return r.results[0]["out"]
```

```python
from contextlib import ExitStack

import concourse.bass as bass
from concourse import mybir

ALU = mybir.AluOpType
ACT = mybir.ActivationFunctionType
AX_X = mybir.AxisListType.X
F32 = mybir.dt.float32
F32R = mybir.dt.float32r
F16 = mybir.dt.float16
BF16 = mybir.dt.bfloat16
I32 = mybir.dt.int32

P = 128
NB, S, H = 2, 1024, 512
NH, D = 16, 32
INTER = 1408
KC = H // P
IT = INTER // P
CH = 512
CC = S // CH
TJ = CH // P
KT = S // P
HEADS = NB * NH
HALF = P // (D // 2)
VW = 3 * D + 1
VP = VW + 1
SCALE = float(1.0 / (D ** 0.5))
LN_EPS = 1e-5
NEG = -1e30
SHIFT = 55.0
SLOTS = 4
K_DOT = 3 * D
K_ALL = K_DOT + 3

S_PIECES = []
for qt in range(KT):
    need = P * (qt + 1)
    if need <= 512:
        S_PIECES.append((qt, 0, max(need, 256), 0))
    else:
        first = 384 if need == 640 else 512
        S_PIECES += [(qt, 0, first, 0), (qt, first, need - first, 1)]
S_PIECES.sort(key=lambda piece: (-piece[2], -piece[0]))
M_ENTRY = 5
S_BANKS = [[piece] for piece in S_PIECES[:-2]] + [S_PIECES[-2:]]
S_BANKS.insert(M_ENTRY, [])
ST_PIECES = [(0, 0, 512, 0), (0, 512, 512, 512), (1, 128, 384, 128), (1, 512, 512, 512),
             (2, 256, 384, 256), (2, 640, 384, 640), (3, 384, 384, 384), (3, 768, 256, 768),
             (4, 512, 512, 512), (5, 640, 384, 640), (6, 768, 256, 768), (7, 768, 256, 896)]
NPC = len(ST_PIECES)
NS = NPC - 1
assert len(S_BANKS) == NPC


def s_before(entry):
    return entry - (entry > M_ENTRY)


LAST_PIECE = [max(i for i, p in enumerate(ST_PIECES) if p[0] == kt) for kt in range(KT)]
P_OFF = [sum(S - P * k for k in range(kt)) for kt in range(KT + 1)]
PV_TERMS = [(kt, qt, part) for kt in range(KT) for qt in range(kt, KT) for part in range(2)]
PV_FIRST, PV_PER_PIECE = 1, 8
assert (NPC - PV_FIRST - 2) * PV_PER_PIECE == len(PV_TERMS)
POOL_KT = 5
DVE_KT = KT - POOL_KT
FFN_COLS = KC * INTER
W_PIECE = 2 * H
FLAG_W = 704
FLAG_N = 3 * FFN_COLS // FLAG_W
assert IT * H == FFN_COLS


def transformer_block(nc, x, wq, wk, wv, wo, bqk, bv, bo, ffn, gs, us, ds, cos, sin, out):
    ctx = ExitStack()
    with ctx:
        def sb(name, shape, dt, scope=ctx):
            return scope.enter_context(nc.sbuf_tensor(name, shape, dt))

        def sem(name):
            return ctx.enter_context(nc.semaphore(name))

        scratch = nc.dram_tensor("qk_scratch", [2, 4, HEADS, D // 2, S], F32, kind="Internal").ap()
        ffn_copy = nc.dram_tensor("ffn_copy", [P, 3 * FFN_COLS], F32, kind="Internal").ap()

        with ExitStack() as under_xT:
            wo_st = sb("wo_st", [P, KC, H], F32, under_xT)
        xT_hi = sb("xT_hi", [P, KC, CH], F32R)
        xT_lo = sb("xT_lo", [P, KC, CH], F32R)
        ident = sb("ident", [P, P], F32)
        ident_b = sb("ident_b", [P, P], BF16)
        mask_kq = sb("mask_kq", [P, P], BF16)
        mask_qk = sb("mask_qk", [P, P], BF16)
        stats = sb("stats", [P, TJ, 6], F32)
        moments = sb("moments", [P, TJ, 2], F32)
        std = sb("std", [P, TJ], F32)
        rstd = sb("rstd", [P, TJ], F32)
        eps = sb("eps", [P, 1], F32)
        bqk_sb = sb("bqk_sb", [P, 8], F32)
        gs_sb = sb("gs_sb", [P, IT], F32)
        us_sb = sb("us_sb", [P, IT], F32)
        flag_sum = sb("flag_sum", [P, FLAG_N], F32)
        flag_part = sb("flag_part", [P, 1], F32)
        flag_all = sb("flag_all", [P, 1], F32)
        flag_int = sb("flag_int", [P, 1], I32)
        with ExitStack() as under_tok:
            rot = sb("rot", [P, 2, 2, CH], F32, under_tok)
            st_hi = sb("st_hi", [P, 2, 2, CH], F32R, under_tok)
            st_lo = sb("st_lo", [P, 2, 2, CH], F32R, under_tok)
            even = sb("even", [P, 2, CH], F32, under_tok)
            odd = sb("odd", [P, 2, CH], F32, under_tok)
        tok = sb("tok", [P, KT, NB, H], F32)
        with ExitStack() as under_wo:
            w_st = sb("w_st", [P, 2, W_PIECE], F32, under_wo)
            cos_sb = sb("cos_sb", [P, S], F32, under_wo)
            sin_sb = sb("sin_sb", [P, S], F32, under_wo)
        wo_hi = sb("wo_hi", [P, KC, H], F32R)
        wo_lo = sb("wo_lo", [P, KC, H], F32R)
        with ExitStack() as stage_ab:
            v_sb = sb("v_sb", [P, KT, HEADS, VP], BF16, stage_ab)
            with ExitStack() as stage_a:
                w_split = [[sb(f"w_{part}{m}", [P, KC, H], F32R, stage_a) for part in ("hi", "lo")] for m in range(3)]
                w_hi, w_lo = [w[0] for w in w_split], [w[1] for w in w_split]
                xst_a = sb("xst_a", [P, CC, TJ, H], F32, stage_a)
                bv_sb = sb("bv_sb", [P, H], F32, stage_a)
                ecos = sb("ecos", [P, CH], F32, stage_a)
                osin = sb("osin", [P, CH], F32, stage_a)
                ocos = sb("ocos", [P, 2, CH], F32, stage_a)
                esin = sb("esin", [P, 2, CH], F32, stage_a)
                v32 = sb("v32", [P, 2, H], F32, stage_a)
                v_rest = sb("v_rest", [P, 2, H], F32, stage_a)
            with ExitStack() as stage_b:
                q_st = sb("q_st", [P, SLOTS, S], F32R, stage_b)
                k_st = sb("k_st", [P, SLOTS, S], F32R, stage_b)
                p32 = sb("p32", [P, P_OFF[KT]], F32, stage_b)
                p_hi = sb("p_hi", [P, 2, P_OFF[KT]], F16, stage_b)
                p_lo = sb("p_lo", [P, 2, P_OFF[KT]], F16, stage_b)
                row_max = sb("row_max", [P, 2, KT, 2], F32, stage_b)
                max8 = sb("max8", [P, KT], F32, stage_b)
                neg_max = sb("neg_max", [P, 2 * KT], F32R, stage_b)
                neg_max_T = sb("neg_max_T", [2 * KT, 2, P], F32, stage_b)
                o_sum = sb("o_sum", [P, KT, D], F32, stage_b)
                o_rec = sb("o_rec", [P, KT], F32, stage_b)
        wg_sb = sb("wg_sb", [P, KC, INTER], F32R)
        wu_sb = sb("wu_sb", [P, KC, INTER], F32R)
        wd_sb = sb("wd_sb", [P, IT, H], F32R)
        xh = sb("xh", [P, KT, NB, H], F32)
        xst_c = sb("xst_c", [P, TJ, H], F32)
        ds_sb = sb("ds_sb", [P, H], F32)
        with ExitStack() as stage_c1:
            xr = sb("xr", [P, CC, TJ, H], F32, stage_c1)
            bo_sb = sb("bo_sb", [P, H], F32, stage_c1)
        with ExitStack() as stage_c2:
            silu = sb("silu", [P, 2, CH], F32, stage_c2)
            hid = sb("hid", [P, 2, CH], F32, stage_c2)
            hid_hi = sb("hid_hi", [P, 3, CH], F32R, stage_c2)
            hid_lo = sb("hid_lo", [P, 3, CH], F32R, stage_c2)
            y_sb = sb("y_sb", [P, TJ, H], F32, stage_c2)

        ps = ctx.enter_context(nc.psum_tensor("ps", [P, 8, 512], F32))
        T_BANK, MM_BANK = 0, 4
        S_BANK, ST_BANK, O_BANK = 0, 3, 6
        RING = 3
        M_BANK = S_BANK + M_ENTRY % RING

        x_in = [sem(f"x_in{g}") for g in range(NB * CC)]
        const_in = sem("const_in")
        w_in = [sem(f"w_in{k}") for k in range(2)]
        ffn_copied = sem("ffn_copied")
        consts = sem("consts")
        w_hi_done = sem("w_hi_done")
        w_lo_done = sem("w_lo_done")
        low_bits = sem("low_bits")
        flag_done = sem("flag_done")
        ln_stats = sem("ln_stats")
        ln_moments = sem("ln_moments")
        ln_std = sem("ln_std")
        ln_rstd = sem("ln_rstd")
        ln_done = sem("ln_done")
        x2_tokens = sem("x2_tokens")
        t_ps = sem("t_ps")
        t_hi = sem("t_hi")
        t_lo = sem("t_lo")
        qk_ps = sem("qk_ps")
        eo_ready = sem("eo_ready")
        rope_prod = sem("rope_prod")
        pool_prod = sem("pool_prod")
        rope_done = sem("rope_done")
        rot_hi = sem("rot_hi")
        rot_lo = sem("rot_lo")
        scr_out = [sem(f"scr_out{k}") for k in range(2)]
        v_ps = sem("v_ps")
        v32_ready = sem("v32_ready")
        v1_ready = sem("v1_ready")
        rest_ready = sem("rest_ready")
        v2_ready = sem("v2_ready")
        v3_ready = sem("v3_ready")
        q_rows = sem("q_rows")
        k_rows = sem("k_rows")
        row_max_init = sem("row_max_init")
        head_in = [sem(f"head_in{k}") for k in range(SLOTS)]
        s_ps = sem("s_ps")
        s_max = sem("s_max")
        max_step = sem("max_step")
        max_ready = sem("max_ready")
        max_T_ps = sem("max_T_ps")
        max_T = sem("max_T")
        max_in = [sem(f"max_in{k}") for k in range(SLOTS)]
        st_ps = sem("st_ps")
        exp_done = sem("exp_done")
        p_hi_done = sem("p_hi_done")
        p_lo_pool = sem("p_lo_pool")
        p_lo_dve = sem("p_lo_dve")
        pv_first = sem("pv_first")
        pv_done = sem("pv_done")
        o_sums = sem("o_sums")
        o_parts = sem("o_parts")
        o_done = sem("o_done")
        wo_in = sem("wo_in")
        wo_hi_done = sem("wo_hi_done")
        wo_lo_done = sem("wo_lo_done")
        c_in = sem("c_in")
        ffn_in = sem("ffn_in")
        xr_in = [sem(f"xr_in{k}") for k in range(NB * CC)]
        xr_ready = sem("xr_ready")
        o_ps = sem("o_ps")
        x2_ready = sem("x2_ready")
        flag_ready = sem("flag_ready")
        g_ps = sem("g_ps")
        u_ps = sem("u_ps")
        silu_ready = sem("silu_ready")
        hid_ready = sem("hid_ready")
        hid_hi_done = sem("hid_hi_done")
        hid_lo_done = sem("hid_lo_done")
        down_ps = sem("down_ps")
        y_scaled = sem("y_scaled")
        y_ready = sem("y_ready")
        y_out = [sem(f"y_out{j}") for j in range(TJ)]

        N_CH = NB * CC
        block = ctx.enter_context(nc.Block())

        def stage_a_done(eng):
            eng.wait_ge(v32_ready, N_CH * TJ)
            eng.wait_ge(v2_ready, N_CH * TJ)
            eng.wait_ge(v3_ready, N_CH * TJ)
            eng.wait_ge(v_ps, N_CH * TJ)
            eng.wait_ge(flag_done, FLAG_N)
            for k in range(2):
                eng.wait_ge(scr_out[k], 64 * 2 * N_CH)

        def stage_b_done(eng):
            eng.wait_ge(pv_done, HEADS)
            eng.wait_ge(o_done, HEADS)
            eng.wait_ge(st_ps, NPC * HEADS)
            eng.wait_ge(s_max, NS * HEADS)
            eng.wait_ge(max_T, HEADS)

        def stage_c1_done(eng):
            eng.wait_ge(x2_ready, N_CH * TJ)

        def chunks(eng):
            with eng.Fori(0, NB) as b:
                for cc in range(CC):
                    yield b, cc, b * CC + cc

        def t_bank(j, c2=False):
            return T_BANK + ((j + 2) % TJ if c2 else j)

        @block.sync
        def _(sp):
            def load_x(dst, b, cc):
                return sp.dma_start(dst[:, cc, :, :], x[b, cc * CH:(cc + 1) * CH, :].rearrange("(j p) h -> p j h", p=P))

            for j in range(TJ):
                sp.dma_start(xst_a[:, 0, j, :], x[0, j * P:(j + 1) * P, :]).then_inc(x_in[0], 16)
            for n in range(6):
                if n >= 2:
                    sp.wait_ge(w_lo_done, n - 1)
                src = (wq, wk, wv)[n // 2][:, n % 2 * W_PIECE:(n % 2 + 1) * W_PIECE]
                sp.dma_start(w_st[:, n % 2, :], src).then_inc(w_in[n % 2], 16)
                if n == 1:
                    sp.dma_start(bqk_sb[:, :], bqk).then_inc(const_in, 16)
                    sp.dma_start(cos_sb[:, :], cos).then_inc(const_in, 16)
                    sp.dma_start(sin_sb[:, :], sin).then_inc(const_in, 16)
                    sp.dma_start(bv_sb[:, :], bv.partition_broadcast(P)).then_inc(const_in, 16)
                    sp.dma_start(gs_sb[:, :], gs).then_inc(const_in, 16)
                    sp.dma_start(us_sb[:, :], us).then_inc(const_in, 16)
                if n == 3:
                    load_x(xst_a, 0, 1).then_inc(x_in[1], 16)
            sp.dma_start(ffn_copy, ffn).then_inc(ffn_copied, 16)
            sp.wait_ge(w_lo_done, 6)

            def load_flag_piece(c, k):
                sp.wait_ge(flag_done, 6 * c + max(k - 1, 0))
                sp.dma_start(w_st[:, k % 2, 0:FLAG_W], ffn[:, bass.ds((6 * c + k) * FLAG_W, FLAG_W)]).then_inc(w_in[k % 2], 16)

            for b, cc, c in chunks(sp):
                load_flag_piece(c, 0)
                load_flag_piece(c, 1)
                for p in range(4):
                    for half, done, st in ((0, rot_hi, st_hi), (1, rot_lo, st_lo)):
                        sp.wait_ge(done, 4 * c + p + 1)
                        for eo in range(2):
                            dst = scratch[p // 2, 2 * half + eo, bass.ds(b * NH + p % 2 * HALF, HALF), :, cc * CH:(cc + 1) * CH]
                            sp.dma_start(dst.rearrange("h i s -> (h i) s"), st[:, p % 2, eo, :].bitcast(F32)).then_inc(scr_out[p % 2], 16)
                    load_flag_piece(c, p + 2)

            sp.wait_ge(qk_ps, 4 * N_CH)
            for k in range(2):
                sp.wait_ge(scr_out[k], 64 * 2 * N_CH)

            def load_head(t, slot):
                q, k = scratch[0], scratch[1]
                at = bass.ds(t, 1)
                hi, both = slice(0, 2), slice(0, 4)
                for dst, rows, src, parts in ((q_st, slice(0, 32), q, hi), (q_st, slice(32, 96), q, both),
                                              (k_st, slice(0, 64), k, both), (k_st, slice(64, 96), k, hi)):
                    sp.dma_start(dst[rows, slot, :].bitcast(F32), src[parts, at, :, :].rearrange("r o i s -> r (o i) s")).then_inc(head_in[slot], 16)

            def load_max(u, slot):
                sp.wait_ge(max_T, u + 1)
                for part in range(2):
                    sp.dma_start(q_st[K_DOT + part:K_DOT + part + 1, slot, :].bitcast(F32), neg_max_T[part * KT:(part + 1) * KT, slot % 2, :]).then_inc(max_in[slot], 16)

            def b_step(t, j, last=False):
                if not (last and j >= SLOTS - 1):
                    load_max(t + 1, (j + 1) % SLOTS)
                if not last:
                    sp.wait_ge(st_ps, NPC * (t + 1))
                    load_head(t + SLOTS, j)

            for t in range(SLOTS):
                load_head(t, t)
            stage_a_done(sp)
            sp.dma_start(wo_st[:, :, :], wo).then_inc(wo_in, 16)
            sp.wait_ge(q_rows, 1)
            load_max(0, 0)
            for t in range(SLOTS):
                b_step(t, t)
            with sp.Fori(1, HEADS // SLOTS - 1) as it:
                for j in range(SLOTS):
                    b_step(it * SLOTS + j, j)
            for j in range(SLOTS):
                b_step(HEADS - SLOTS + j, j, last=True)

            stage_b_done(sp)
            sp.dma_start(bo_sb[:, :], bo.partition_broadcast(P)).then_inc(c_in, 16)
            sp.dma_start(ds_sb[:, :], ds.partition_broadcast(P)).then_inc(c_in, 16)
            load_x(xr, 0, 0).then_inc(xr_in[0], 16)
            load_x(xr, 0, 1).then_inc(xr_in[1], 16)
            sp.wait_ge(ffn_copied, 16)
            for m, dst in enumerate((wg_sb, wu_sb, wd_sb)):
                sp.dma_start(dst[:, :, :].rearrange("p a n -> p (a n)").bitcast(F32), ffn_copy[:, m * FFN_COLS:(m + 1) * FFN_COLS]).then_inc(ffn_in, 16)
            for cc in range(CC):
                sp.wait_ge(x2_ready, TJ * (cc + 1))
                load_x(xr, 1, cc).then_inc(xr_in[CC + cc], 16)
            for b, cc, c in chunks(sp):
                for j in range(TJ):
                    sp.wait_ge(y_ready, TJ * c + j + 1)
                    sp.dma_start(out[bass.ds(b, 1), cc * CH + j * P:cc * CH + (j + 1) * P, :].rearrange("o p h -> (o p) h"), y_sb[:, j, :]).then_inc(y_out[j], 16)
            for j in range(TJ):
                sp.wait_ge(y_out[j], 16 * N_CH)

        @block.gpsimd
        def _(pool):
            pool.memset(ident[:, :], 0.0)
            pool.memset(ident_b[:, :], 0.0)
            pool.memset(mask_kq[:, :], 0.0)
            pool.memset(mask_qk[:, :], 0.0)
            pool.memset(eps[:, :], LN_EPS)
            pool.memset(v_sb[:, :, :, 3 * D:VP], 1.0).then_inc(consts, 1)
            pool.wait_ge(consts, 1)
            for m in (ident, ident_b):
                pool.affine_select(out=m[:, :], in_=m[:, :], compare_op=ALU.not_equal, fill=1.0, base=0,
                                   pattern=[[-1, P]], channel_multiplier=1)
            pool.affine_select(out=mask_kq[:, :], in_=mask_kq[:, :], compare_op=ALU.is_ge, fill=NEG, base=0,
                               pattern=[[1, P]], channel_multiplier=-1)
            pool.affine_select(out=mask_qk[:, :], in_=mask_qk[:, :], compare_op=ALU.is_ge, fill=NEG, base=0,
                               pattern=[[-1, P]], channel_multiplier=1).then_inc(consts, 1)
            pool.wait_ge(const_in, 96)

            for b, cc, c in chunks(pool):
                pos = slice(cc * CH, (cc + 1) * CH)
                for p in range(4):
                    n = 4 * c + p
                    pool.wait_ge(eo_ready, n + 1)
                    pool.wait_ge(rope_done, 4 * c + max(p - 1, 0))
                    pool.tensor_tensor(ocos[:, p % 2, :], odd[:, p % 2, :], cos_sb[:, pos], ALU.mult)
                    pool.tensor_tensor(esin[:, p % 2, :], even[:, p % 2, :], sin_sb[:, pos], ALU.mult).then_inc(pool_prod, 1)

                def rest(j):
                    pool.wait_ge(v1_ready, TJ * c + j + 1)
                    pool.wait_ge(v2_ready, TJ * c + max(j - 1, 0))
                    pool.wait_ge(v3_ready, TJ * c + max(j - 1, 0))
                    v1 = v_sb[:, cc * TJ + j, bass.ds(b * NH, NH), 0:D]
                    pool.tensor_tensor(v_rest[:, j % 2, :].rearrange("p (h d) -> p h d", d=D),
                                       v32[:, j % 2, :].rearrange("p (h d) -> p h d", d=D), v1, ALU.subtract).then_inc(rest_ready, 1)

                def third(j):
                    pool.wait_ge(v2_ready, TJ * c + j + 1)
                    v2 = v_sb[:, cc * TJ + j, bass.ds(b * NH, NH), D:2 * D]
                    v3 = v_sb[:, cc * TJ + j, bass.ds(b * NH, NH), 2 * D:3 * D]
                    pool.tensor_tensor(v3, v_rest[:, j % 2, :].rearrange("p (h d) -> p h d", d=D), v2, ALU.subtract).then_inc(v3_ready, 1)

                rest(0)
                rest(1)
                third(0)
                rest(2)
                third(1)
                rest(3)
                third(2)
                third(3)

            pool.wait_ge(v3_ready, N_CH * TJ)
            pool.memset(q_st[K_DOT:P, :, :].bitcast(F32), SHIFT).then_inc(q_rows, 1)
            pool.wait_ge(q_rows, 1)
            pool.memset(k_st[K_DOT:P, :, :].bitcast(F32), 1.0).then_inc(k_rows, 1)
            pool.wait_ge(k_rows, 1)
            stage_a_done(pool)

            def b_step(t, j):
                for kt in range(POOL_KT):
                    pool.wait_ge(p_hi_done, KT * t + kt + 1)
                    cols = slice(P_OFF[kt], P_OFF[kt + 1])
                    pool.tensor_tensor(p_lo[:, j % 2, cols], p32[:, cols], p_hi[:, j % 2, cols], ALU.subtract).then_inc(p_lo_pool, 1)

            with pool.Fori(0, HEADS // SLOTS) as it:
                for j in range(SLOTS):
                    b_step(it * SLOTS + j, j)

            stage_b_done(pool)
            pool.wait_ge(c_in, 32)
            for c in range(N_CH):
                pool.wait_ge(xr_in[c], 16)
                for j in range(TJ):
                    xt = xr[:, c % CC, j, :]
                    pool.tensor_tensor(xt, xt, bo_sb[:, :], ALU.add).then_inc(xr_ready, 1)
                if c == 0:
                    pool.wait_ge(flag_done, FLAG_N + 1)
                    pool.partition_all_reduce(flag_all[:, :], flag_part[:, :], P, bass.bass_isa.ReduceOp.max).then_inc(flag_ready, 1)
                    pool.wait_ge(flag_ready, 1)
                    pool.tensor_copy(flag_int[:, :], flag_all[:, :]).then_inc(flag_ready, 1)

            stage_c1_done(pool)
            for b, cc, c in chunks(pool):
                for i in range(IT):
                    pool.wait_ge(hid_hi_done, IT * c + i + 1)
                    pool.wait_ge(down_ps, IT * c + max(i - 2, 0))
                    pool.tensor_tensor(hid_lo[:, i % 3, :], hid[:, i % 2, :], hid_hi[:, i % 3, :].bitcast(F32), ALU.subtract).then_inc(hid_lo_done, 1)
                for j in range(TJ):
                    pool.wait_ge(y_scaled, TJ * c + j + 1)
                    pool.tensor_tensor(y_sb[:, j, :], y_sb[:, j, :], tok[:, cc * TJ + j, bass.ds(b, 1), :].rearrange("p o h -> p (o h)"), ALU.add).then_inc(y_ready, 1)

        @block.scalar
        def _(act):
            def std_of(n):
                act.wait_ge(ln_moments, n + 1)
                act.activation(std[:, :], moments[:, :, 1], ACT.Sqrt, bias=eps[:, 0:1]).then_inc(ln_std, 1)

            def transposed_hi(n, j, c2=False):
                act.wait_ge(t_ps, TJ * n + j + 1)
                act.copy(xT_hi[:, :, j * P:(j + 1) * P], ps[:, t_bank(j, c2), :].rearrange("p (k t) -> p k t", t=P)).then_inc(t_hi, 1)

            act.wait_ge(consts, 2)
            std_of(0)

            def weight_hi(n):
                m, cols = n // 2, slice(n % 2 * 2, n % 2 * 2 + 2)
                act.wait_ge(w_in[n % 2], 16 * (n // 2 + 1))
                act.copy(w_hi[m][:, cols, :].rearrange("p a n -> p (a n)"), w_st[:, n % 2, :]).then_inc(w_hi_done, 1)

            weight_hi(0)
            for j in range(TJ):
                transposed_hi(0, j)
            for n in range(1, 6):
                weight_hi(n)
            act.wait_ge(const_in, 96)
            for c in range(N_CH):
                b, cc = divmod(c, CC)

                def evacuate(p):
                    n = 4 * c + p
                    act.wait_ge(qk_ps, n + 1)
                    if n >= 2:
                        act.wait_ge(rope_done, n - 1)
                    bank = MM_BANK + 2 * (p % 2)
                    act.activation(even[:, p % 2, :], ps[:, bank, :], ACT.Identity, bias=bqk_sb[:, 2 * p:2 * p + 1])
                    act.activation(odd[:, p % 2, :], ps[:, bank + 1, :], ACT.Identity, bias=bqk_sb[:, 2 * p + 1:2 * p + 2]).then_inc(eo_ready, 1)

                def high(p):
                    n = 4 * c + p
                    act.wait_ge(rope_done, n + 1)
                    if n >= 2:
                        act.wait_ge(scr_out[p % 2], 64 * (n // 2))
                    act.copy(st_hi[:, p % 2, :, :].rearrange("p e s -> p (e s)"),
                             rot[:, p % 2, :, :].rearrange("p e s -> p (e s)")).then_inc(rot_hi, 1)

                def test_piece(k):
                    f = 6 * c + k
                    act.wait_ge(low_bits, f + 1)
                    act.activation(w_st[:, k % 2, 0:FLAG_W], w_st[:, k % 2, 0:FLAG_W].bitcast(I32), ACT.Identity,
                                   accum_out=flag_sum[:, f:f + 1]).then_inc(flag_done, 1)

                if 2 <= c + 1 < N_CH:
                    act.wait_ge(t_ps, TJ * c)
                    nb, ncc = divmod(c + 1, CC)
                    act.dma_start(xst_a[:, ncc, :, :], x[nb, ncc * CH:(ncc + 1) * CH, :].rearrange("(j p) h -> p j h", p=P)).then_inc(x_in[c + 1], 16)
                evacuate(0)
                test_piece(0)
                evacuate(1)
                high(0)
                test_piece(1)
                if c + 1 < N_CH:
                    std_of(c + 1)
                evacuate(2)
                high(1)
                test_piece(2)
                evacuate(3)
                high(2)
                test_piece(3)

                def v_part(j, part, src, ready, done):
                    act.wait_ge(ready, TJ * c + j + 1)
                    act.copy(v_sb[:, cc * TJ + j, b * NH:(b + 1) * NH, part * D:(part + 1) * D],
                             src[:, j % 2, :].rearrange("p (h d) -> p h d", d=D)).then_inc(done, 1)

                def next_tile(j):
                    if c + 1 < N_CH:
                        act.wait_ge(v_ps, TJ * c + j + 1)
                        transposed_hi(c + 1, j)

                v_part(0, 0, v32, v32_ready, v1_ready)
                high(3)
                v_part(1, 0, v32, v32_ready, v1_ready)
                next_tile(0)
                v_part(0, 1, v_rest, rest_ready, v2_ready)
                v_part(2, 0, v32, v32_ready, v1_ready)
                test_piece(4)
                next_tile(1)
                v_part(1, 1, v_rest, rest_ready, v2_ready)
                next_tile(2)
                next_tile(3)
                v_part(3, 0, v32, v32_ready, v1_ready)
                test_piece(5)
                v_part(2, 1, v_rest, rest_ready, v2_ready)
                v_part(3, 1, v_rest, rest_ready, v2_ready)

            stage_a_done(act)

            def exp_piece(t, j, i):
                kt, q0, w, keep = ST_PIECES[i]
                act.wait_ge(st_ps, NPC * t + i + 1)
                at = P_OFF[kt] + keep - P * kt
                act.activation(p32[:, at:at + q0 + w - keep], ps[:, ST_BANK + i % RING, keep - q0:w], ACT.Exp, scale=SCALE).then_inc(exp_done, 1)

            def b_step(t, j, it, first=False, last=False):
                def exps(kt):
                    if not (first and j == 0):
                        if kt < POOL_KT:
                            act.wait_ge(p_lo_pool, POOL_KT * (t - 1) + kt + 1)
                        else:
                            act.wait_ge(p_lo_dve, DVE_KT * (t - 1) + kt - POOL_KT + 1)
                    for i in range(NPC):
                        if ST_PIECES[i][0] == kt:
                            exp_piece(t, j, i)

                def high(kt):
                    act.wait_ge(exp_done, NPC * t + LAST_PIECE[kt] + 1)
                    cols = slice(P_OFF[kt], P_OFF[kt + 1])
                    act.copy(p_hi[:, j % 2, cols], p32[:, cols]).then_inc(p_hi_done, 1)

                def next_max():
                    act.wait_ge(max_T_ps, t + 2)
                    if not (first and j < 1):
                        act.wait_ge(max_in[(j - 1) % SLOTS], 32 * (it + (j - 1) // SLOTS + 1))
                    act.copy(neg_max_T[:, (j + 1) % 2, :], ps[0:2 * KT, M_BANK, 0:P]).then_inc(max_T, 1)

                if not (first and j < 2):
                    act.wait_ge(pv_done, t - 1)
                for kt in range(KT):
                    exps(kt)
                    if kt > 0:
                        high(kt - 1)
                    if kt == 3 and not (last and j == SLOTS - 1):
                        next_max()
                high(KT - 1)
                if first and j == 1:
                    act.wait_ge(wo_in, 16)
                    act.copy(wo_hi[:, :, :], wo_st[:, :, :]).then_inc(wo_hi_done, 1)

            act.wait_ge(max_T_ps, 1)
            act.copy(neg_max_T[:, 0, :], ps[0:2 * KT, M_BANK, 0:P]).then_inc(max_T, 1)
            for j in range(SLOTS):
                b_step(j, j, 0, first=True)
            with act.Fori(1, HEADS // SLOTS - 1) as it:
                for j in range(SLOTS):
                    b_step(it * SLOTS + j, j, it)
            for j in range(SLOTS):
                b_step(HEADS - SLOTS + j, j, HEADS // SLOTS - 1, last=True)

            stage_b_done(act)
            act.wait_ge(wo_lo_done, 1)

            def copy_tiles(c):
                b, cc = divmod(c, CC)
                act.wait_ge(ln_done, N_CH + c + 1)
                act.wait_ge(t_ps, TJ * (2 * N_CH + c))
                for j in range(TJ):
                    act.copy(xst_c[:, j, :], xh[:, cc * TJ + j, b, :]).then_inc(x2_tokens, 1)

            for j in range(TJ):
                transposed_hi(N_CH, j)
            for c in range(N_CH):
                if c + 1 < N_CH:
                    for j in range(TJ):
                        act.wait_ge(o_ps, TJ * c + j + 1)
                        transposed_hi(N_CH + c + 1, j)
                if c == N_CH - 2:
                    copy_tiles(0)
                std_of(N_CH + c)

            act.wait_ge(o_ps, N_CH * TJ)
            for j in range(TJ):
                transposed_hi(2 * N_CH, j, c2=True)
            stage_c1_done(act)
            for c in range(N_CH):
                if c + 1 < N_CH:
                    copy_tiles(c + 1)
                for i in range(IT):
                    n = IT * c + i
                    act.wait_ge(g_ps, n + 1)
                    act.wait_ge(hid_ready, IT * c + max(i - 1, 0))
                    act.activation(silu[:, i % 2, :], ps[:, T_BANK + 2 * (i % 2), :], ACT.Silu, scale=gs_sb[:, i:i + 1]).then_inc(silu_ready, 1)
                    act.wait_ge(hid_ready, n + 1)
                    act.wait_ge(down_ps, IT * c + max(i - 2, 0))
                    act.copy(hid_hi[:, i % 3, :], hid[:, i % 2, :]).then_inc(hid_hi_done, 1)
                if c + 1 < N_CH:
                    for j in range(TJ):
                        transposed_hi(2 * N_CH + c + 1, j, c2=True)

        @block.vector
        def _(dve):
            def ln_first(n, tiles):
                for j in range(TJ):
                    ins = dve.bn_stats(stats[:, j, :], tiles[j])
                ins.then_inc(ln_stats, 1)
                dve.wait_ge(ln_stats, n + 1)
                for j in range(TJ):
                    ins = dve.bn_aggr(moments[:, j, :], stats[:, j, :])
                ins.then_inc(ln_moments, 1)

            def ln_second(n, tiles, outs):
                dve.wait_ge(ln_std, n + 1)
                dve.reciprocal(rstd[:, :], std[:, :]).then_inc(ln_rstd, 1)
                dve.wait_ge(ln_rstd, n + 1)
                for j in range(TJ):
                    ins = dve.tensor_scalar(outs[j], tiles[j], moments[:, j, 0:1], rstd[:, j:j + 1], ALU.subtract, ALU.mult)
                ins.then_inc(ln_done, 1)

            def transposed_lo(n, j, c2=False):
                tile = slice(j * P, (j + 1) * P)
                dve.wait_ge(t_hi, TJ * n + j + 1)
                dve.tensor_tensor(xT_lo[:, :, tile], ps[:, t_bank(j, c2), :].rearrange("p (k t) -> p k t", t=P),
                                  xT_hi[:, :, tile].bitcast(F32), ALU.subtract).then_inc(t_lo, 1)

            def a_tiles(c):
                return [xst_a[:, c % CC, j, :] for j in range(TJ)]

            def weight_lo(n):
                m, cols = n // 2, slice(n % 2 * 2, n % 2 * 2 + 2)
                dve.wait_ge(w_hi_done, n + 1)
                dve.tensor_tensor(w_lo[m][:, cols, :].rearrange("p a n -> p (a n)"), w_st[:, n % 2, :],
                                  w_hi[m][:, cols, :].rearrange("p a n -> p (a n)").bitcast(F32), ALU.subtract).then_inc(w_lo_done, 1)

            dve.wait_ge(x_in[0], 16 * TJ)
            ln_first(0, a_tiles(0))
            ln_second(0, a_tiles(0), a_tiles(0))
            weight_lo(0)
            for j in range(TJ):
                transposed_lo(0, j)
            for n in range(1, 6):
                weight_lo(n)
            dve.wait_ge(const_in, 96)
            for c in range(N_CH):
                cc = c % CC
                pos = slice(cc * CH, (cc + 1) * CH)

                def rotate(p):
                    n = 4 * c + p
                    dve.wait_ge(eo_ready, n + 1)
                    if n >= 1:
                        dve.wait_ge(rope_done, n)
                    dve.tensor_tensor(ecos[:, :], even[:, p % 2, :], cos_sb[:, pos], ALU.mult)
                    dve.tensor_tensor(osin[:, :], odd[:, p % 2, :], sin_sb[:, pos], ALU.mult).then_inc(rope_prod, 1)
                    dve.wait_ge(rope_prod, n + 1)
                    if n >= 2:
                        dve.wait_ge(rot_hi, n - 1)
                    dve.tensor_tensor(rot[:, p % 2, 0, :], ecos[:, :], osin[:, :], ALU.subtract)
                    dve.wait_ge(pool_prod, n + 1)
                    dve.tensor_tensor(rot[:, p % 2, 1, :], ocos[:, p % 2, :], esin[:, p % 2, :], ALU.add).then_inc(rope_done, 1)

                def low(p):
                    n = 4 * c + p
                    dve.wait_ge(rot_hi, n + 1)
                    dve.tensor_tensor(st_lo[:, p % 2, :, :].rearrange("p e s -> p (e s)"), rot[:, p % 2, :, :].rearrange("p e s -> p (e s)"),
                                      st_hi[:, p % 2, :, :].rearrange("p e s -> p (e s)").bitcast(F32), ALU.subtract).then_inc(rot_lo, 1)

                def test_piece(k):
                    f = 6 * c + k
                    piece = w_st[:, k % 2, 0:FLAG_W].bitcast(I32)
                    dve.wait_ge(w_in[k % 2], 16 * (3 + f // 2 + 1))
                    dve.tensor_single_scalar(piece, piece, (1 << 12) - 1, ALU.bitwise_and).then_inc(low_bits, 1)

                def v_bias(j):
                    idx = TJ * c + j
                    dve.wait_ge(v_ps, idx + 1)
                    if idx >= 2:
                        dve.wait_ge(rest_ready, idx - 1)
                    dve.tensor_tensor(v32[:, j % 2, :], ps[:, MM_BANK + j, :], bv_sb[:, :], ALU.add).then_inc(v32_ready, 1)

                def next_tile(j):
                    if c + 1 < N_CH:
                        transposed_lo(c + 1, j)

                test_piece(0)
                test_piece(1)
                rotate(0)
                if c + 1 < N_CH:
                    dve.wait_ge(x_in[c + 1], 16)
                    ln_first(c + 1, a_tiles(c + 1))
                low(0)
                rotate(1)
                if c + 1 < N_CH:
                    ln_second(c + 1, a_tiles(c + 1), a_tiles(c + 1))
                low(1)
                test_piece(2)
                rotate(2)
                low(2)
                test_piece(3)
                test_piece(4)
                rotate(3)
                v_bias(0)
                low(3)
                v_bias(1)
                next_tile(0)
                v_bias(2)
                next_tile(1)
                test_piece(5)
                next_tile(2)
                next_tile(3)
                v_bias(3)
            dve.wait_ge(flag_done, FLAG_N)
            dve.tensor_reduce(flag_part[:, :], flag_sum[:, :], AX_X, ALU.max).then_inc(flag_done, 1)

            stage_a_done(dve)
            dve.memset(row_max[:, :, :, :], NEG).then_inc(row_max_init, 1)
            dve.wait_ge(row_max_init, 1)

            def max_piece(u, half, i):
                if i != M_ENTRY:
                    dve.wait_ge(s_ps, NS * u + s_before(i) + 1)
                    col = 0
                    for qt, k0, w, part in S_BANKS[i]:
                        kept = min(w, P * (qt + 1) - k0)
                        ins = dve.tensor_reduce(row_max[:, half, qt, part:part + 1], ps[:, S_BANK + i % RING, col:col + kept], AX_X, ALU.max)
                        col += w
                    ins.then_inc(s_max, 1)

            def negate_max(u, half, step):
                if step == 0:
                    dve.wait_ge(s_max, NS * (u + 1))
                    dve.tensor_reduce(max8[:, :], row_max[:, half, :, :], AX_X, ALU.max).then_inc(max_step, 1)
                elif step == 1:
                    dve.wait_ge(max_step, 2 * u + 1)
                    dve.wait_ge(max_T_ps, u)
                    dve.tensor_scalar(neg_max[:, 0:KT], max8[:, :], -1.0, None, ALU.mult).then_inc(max_step, 1)
                else:
                    dve.wait_ge(max_step, 2 * u + 2)
                    dve.scalar_tensor_tensor(out=neg_max[:, KT:2 * KT], in0=max8[:, :], scalar=-1.0, in1=neg_max[:, 0:KT].bitcast(F32),
                                             op0=ALU.mult, op1=ALU.subtract).then_inc(max_ready, 1)

            def low(r, half, kt):
                dve.wait_ge(p_hi_done, KT * r + kt + 1)
                cols = slice(P_OFF[kt], P_OFF[kt + 1])
                dve.tensor_tensor(p_lo[:, half, cols], p32[:, cols], p_hi[:, half, cols], ALU.subtract).then_inc(p_lo_dve, 1)

            def output_parts(r, g):
                o = ps[:, O_BANK + g, 0:4 * VW].rearrange("p (q e) -> p q e", e=VW)
                q4 = slice(4 * g, 4 * g + 4)
                dve.wait_ge(o_done, r)
                dve.wait_ge(pv_first if g == 0 else pv_done, r + 1)
                dve.tensor_reduce(o_sum[:, q4, :], o[:, :, 0:3 * D].rearrange("p q (s d) -> p q d s", d=D), AX_X, ALU.add).then_inc(o_sums, 1)
                dve.reciprocal(o_rec[:, q4], o[:, :, 3 * D]).then_inc(o_parts, 1)

            def output(r):
                dve.wait_ge(o_parts, 2 * (r + 1))
                dst = tok[:, :, :, :].rearrange("p k b (h d) -> p k (b h) d", d=D)[:, :, bass.ds(r, 1), :].rearrange("p k o d -> p k (o d)")
                dve.tensor_tensor(dst, o_sum[:, :, :], o_rec[:, :].unsqueeze(2).broadcast_to([P, KT, D]), ALU.mult).then_inc(o_done, 1)

            def b_step(t, j, scores=True, negate=True, before=True):
                for i in range(NPC):
                    if scores:
                        max_piece(t + 2, j % 2, i)
                    if negate and i < 3:
                        negate_max(t + 1, (j + 1) % 2, i)
                    if before:
                        if POOL_KT <= i < KT:
                            low(t - 1, (j + 1) % 2, i)
                        elif i == 8:
                            output_parts(t - 1, 0)
                        elif i == 10:
                            output_parts(t - 1, 1)
                        elif i == 11:
                            output(t - 1)

            b_step(-2, 0, negate=False, before=False)
            b_step(-1, 1, before=False)
            for j in range(SLOTS):
                b_step(j, j, before=j > 0)
                if j == 1:
                    dve.wait_ge(wo_hi_done, 1)
                    dve.tensor_tensor(wo_lo[:, :, :], wo_st[:, :, :], wo_hi[:, :, :].bitcast(F32), ALU.subtract).then_inc(wo_lo_done, 1)
            with dve.Fori(1, HEADS // SLOTS - 1) as it:
                for j in range(SLOTS):
                    b_step(it * SLOTS + j, j)
            for j in range(SLOTS + 1):
                t = HEADS - SLOTS + j
                b_step(t, j, scores=t + 2 < HEADS, negate=t + 1 < HEADS)

            stage_b_done(dve)

            def c_tiles(src, c):
                b, cc = divmod(c, CC)
                return [src[:, cc * TJ + j, b, :] for j in range(TJ)]

            for j in range(TJ):
                transposed_lo(N_CH, j)
            for c in range(N_CH):
                for j, x2 in enumerate(c_tiles(tok, c)):
                    dve.wait_ge(o_ps, TJ * c + j + 1)
                    dve.wait_ge(xr_ready, TJ * c + j + 1)
                    dve.tensor_tensor(x2, ps[:, MM_BANK + j, :], xr[:, c % CC, j, :], ALU.add).then_inc(x2_ready, 1)
                    if c + 1 < N_CH:
                        transposed_lo(N_CH + c + 1, j)
                if c > 0:
                    ln_second(N_CH + c - 1, c_tiles(tok, c - 1), c_tiles(xh, c - 1))
                dve.wait_ge(x2_ready, TJ * (c + 1))
                ln_first(N_CH + c, c_tiles(tok, c))
            for j in range(TJ):
                transposed_lo(2 * N_CH, j, c2=True)
            ln_second(2 * N_CH - 1, c_tiles(tok, N_CH - 1), c_tiles(xh, N_CH - 1))

            stage_c1_done(dve)
            dve.wait_ge(c_in, 32)
            for c in range(N_CH):
                for i in range(IT):
                    n = IT * c + i
                    dve.wait_ge(u_ps, n + 1)
                    dve.wait_ge(silu_ready, n + 1)
                    dve.wait_ge(hid_lo_done, IT * c + max(i - 1, 0))
                    dve.scalar_tensor_tensor(out=hid[:, i % 2, :], in0=ps[:, T_BANK + 2 * (i % 2) + 1, :], scalar=us_sb[:, i:i + 1],
                                             in1=silu[:, i % 2, :], op0=ALU.mult, op1=ALU.mult).then_inc(hid_ready, 1)
                if c + 1 < N_CH:
                    for j in range(TJ):
                        transposed_lo(2 * N_CH + c + 1, j, c2=True)
                for j in range(TJ):
                    if j == 0:
                        dve.wait_ge(down_ps, IT * (c + 1))
                    dve.wait_ge(y_out[j], 16 * c)
                    dve.tensor_tensor(y_sb[:, j, :], ps[:, MM_BANK + j, :], ds_sb[:, :], ALU.mult).then_inc(y_scaled, 1)

        @block.tensor
        def _(pe):
            def transpose_tile(j, tokens, free, c2=False):
                pe.wait_ge(t_lo, free)
                for kc in range(KC):
                    ins = pe.transpose(ps[:, t_bank(j, c2), kc * P:(kc + 1) * P], tokens[:, kc * P:(kc + 1) * P], ident[:, :])
                ins.then_inc(t_ps, 1)

            def product(dst, terms):
                for k, (w, m) in enumerate(terms):
                    ins = pe.matmul(dst, w, m, start=(k == 0), stop=(k == len(terms) - 1))
                return ins

            THREE = ((0, xT_hi), (1, xT_hi), (0, xT_lo))
            pe.wait_ge(consts, 2)
            for b, cc, c in chunks(pe):
                if cc == 0:
                    pe.wait_ge(ln_done, c + 1)
                    for j in range(TJ):
                        transpose_tile(j, xst_a[:, cc, j, :], TJ * c)
                pe.wait_ge(t_lo, TJ * (c + 1))
                for p in range(4):
                    pe.wait_ge(w_lo_done, 2 if p < 2 else 4)
                    if p == 0:
                        pe.wait_ge(v32_ready, TJ * c - (2 if cc > 0 else 0))
                    elif p == 1:
                        pe.wait_ge(v32_ready, TJ * c)
                    else:
                        pe.wait_ge(eo_ready, 4 * c + p - 1)
                    m, half = p // 2, p % 2
                    for eo in range(2):
                        cols = slice((2 * half + eo) * P, (2 * half + eo + 1) * P)
                        ins = product(ps[:, MM_BANK + 2 * half + eo, :],
                                      [(w_split[m][part][:, kc, cols], xT[:, kc, :]) for part, xT in THREE for kc in range(KC)])
                    ins.then_inc(qk_ps, 1)
                pe.wait_ge(w_lo_done, 6)
                for j in range(TJ):
                    pe.wait_ge(eo_ready, 4 * c + 3 + j // 2)
                    tile = slice(j * P, (j + 1) * P)
                    product(ps[:, MM_BANK + j, :],
                            [(xT[:, kc, tile], w_split[2][part][:, kc, :]) for part, xT in THREE for kc in range(KC)]).then_inc(v_ps, 1)
                    if cc == 0 and j >= 1:
                        if j == 1:
                            pe.wait_ge(ln_done, c + 2)
                        for k in range(j - 1, TJ if j == TJ - 1 else j):
                            transpose_tile(k, xst_a[:, 1, k, :], TJ * c + k + 1)

            pe.wait_ge(t_lo, TJ * N_CH)

            def score_bank(u, slot, uses, i, first=False):
                if i == 0:
                    pe.wait_ge(head_in[slot], 64 * uses)
                if i == M_ENTRY + RING and not first:
                    pe.wait_ge(max_T, u)
                elif i == M_ENTRY + RING:
                    pe.wait_ge(s_max, s_before(M_ENTRY - RING) + 1)
                elif i >= RING:
                    pe.wait_ge(s_max, NS * u + s_before(i - RING) + 1)
                elif not first:
                    pe.wait_ge(s_max, NS * u - RING + i + 1)
                col = 0
                for qt, k0, w, _ in S_BANKS[i]:
                    dst = ps[:, S_BANK + i % RING, col:col + w]
                    diagonal = k0 + w > P * qt
                    ins = pe.matmul(dst, q_st[0:K_DOT, slot, qt * P:(qt + 1) * P], k_st[0:K_DOT, slot, k0:k0 + w],
                                    start=True, stop=not diagonal)
                    if diagonal:
                        d0 = P * qt - k0
                        ins = pe.matmul(dst[:, d0:d0 + P], ident_b[:, :], mask_qk[:, :], start=False, stop=True)
                    col += w
                ins.then_inc(s_ps, 1)

            def transpose_max(v, first=False, scores=True):
                pe.wait_ge(max_ready, v + 1)
                if scores:
                    pe.wait_ge(s_max, NS * (v + 1) + s_before(M_ENTRY - RING) + 1)
                if not first:
                    pe.wait_ge(max_T, v)
                pe.transpose(ps[0:2 * KT, M_BANK, 0:P], neg_max[:, :].bitcast(F32), ident[:, :]).then_inc(max_T_ps, 1)

            def shifted_piece(t, slot, uses, i, first=False):
                kt, q0, w, keep = ST_PIECES[i]
                if i == 0:
                    pe.wait_ge(max_in[slot], 32 * uses)
                if not (first and i < RING):
                    pe.wait_ge(exp_done, NPC * t + i - RING + 1)
                diagonal = i == 0 or ST_PIECES[i - 1][0] != kt
                dst = ps[:, ST_BANK + i % RING, :]
                ins = pe.matmul(dst[:, 0:w], k_st[0:K_ALL, slot, kt * P:(kt + 1) * P], q_st[0:K_ALL, slot, q0:q0 + w],
                                start=True, stop=not diagonal)
                if diagonal:
                    d0 = P * kt - q0
                    ins = pe.matmul(dst[:, d0:d0 + P], ident_b[:, :], mask_kq[:, :], start=False, stop=True)
                ins.then_inc(st_ps, 1)

            def output_products(r, half, n, first=False):
                for kt, qt, part in PV_TERMS[n * PV_PER_PIECE:(n + 1) * PV_PER_PIECE]:
                    if qt == kt and part == 0:
                        pe.wait_ge(p_hi_done, KT * r + kt + 1)
                        if kt < POOL_KT:
                            pe.wait_ge(p_lo_pool, POOL_KT * r + kt + 1)
                        else:
                            pe.wait_ge(p_lo_dve, DVE_KT * r + kt - POOL_KT + 1)
                    opens = kt == 0 and qt % 4 == 0 and part == 0
                    if opens and not first:
                        pe.wait_ge(o_parts, 2 * r - 1 + qt // 4)
                    at = P_OFF[kt] + (qt - kt) * P
                    ins = pe.matmul(ps[:, O_BANK + qt // 4, qt % 4 * VW:(qt % 4 + 1) * VW], (p_hi, p_lo)[part][:, half, at:at + P],
                                    v_sb[:, kt, bass.ds(r, 1), 0:VW].rearrange("p o e -> p (o e)"),
                                    start=opens, stop=(kt == qt and part == 1), skip_group_check=True)
                    if part == 1 and (kt, qt) in ((3, 3), (KT - 1, KT - 1)):
                        ins.then_inc(pv_first if qt == 3 else pv_done, 1)

            def b_step(t, j, it, scores=True, maxima=True, shifted=True, before=True):
                for i in range(NPC):
                    if i == M_ENTRY and maxima:
                        transpose_max(t + 1, first=not shifted, scores=scores)
                    elif i != M_ENTRY and scores:
                        score_bank(t + 2, (j + 2) % SLOTS, it + (j + 2) // SLOTS + 1, i, first=not shifted and not maxima)
                    if shifted:
                        shifted_piece(t, j, it + 1, i, first=not before)
                    if before and 0 <= i - PV_FIRST < len(PV_TERMS) // PV_PER_PIECE:
                        output_products(t - 1, (j + 1) % 2, i - PV_FIRST, first=(it == 0 and j == 1) if type(it) is int else False)

            b_step(-2, 2, -1, maxima=False, shifted=False, before=False)
            b_step(-1, 3, -1, shifted=False, before=False)
            pe.wait_ge(q_rows, 1)
            pe.wait_ge(k_rows, 1)
            pe.wait_ge(v32_ready, N_CH * TJ)
            pe.wait_ge(v2_ready, N_CH * TJ)
            pe.wait_ge(v3_ready, N_CH * TJ)
            for j in range(SLOTS):
                b_step(j, j, 0, before=j > 0)
            with pe.Fori(1, HEADS // SLOTS - 1) as it:
                for j in range(SLOTS):
                    b_step(it * SLOTS + j, j, it)
            for j in range(SLOTS + 1):
                t = HEADS - SLOTS + j
                b_step(t, j, HEADS // SLOTS - 1, scores=t + 2 < HEADS, maxima=t + 1 < HEADS, shifted=t < HEADS)

            stage_b_done(pe)
            pe.wait_ge(wo_lo_done, 1)

            def tokens(c, j):
                b, cc = divmod(c, CC)
                return tok[:, cc * TJ + j, b, :]

            for j in range(TJ):
                transpose_tile(j, tokens(0, j), TJ * N_CH)
            for c in range(N_CH):
                for j in range(TJ):
                    tile = slice(j * P, (j + 1) * P)
                    if c > 0:
                        pe.wait_ge(x2_ready, TJ * (c - 1) + j + 1)
                    pe.wait_ge(t_lo, TJ * (N_CH + c) + j + 1)
                    product(ps[:, MM_BANK + j, :],
                            [(xT[:, kc, tile], (wo_hi, wo_lo)[part][:, kc, :]) for part, xT in THREE for kc in range(KC)]).then_inc(o_ps, 1)
                    if c + 1 < N_CH:
                        transpose_tile(j, tokens(c + 1, j), TJ * (N_CH + c) + j + 1)

            def ffn_products(dt):
                def t(ap):
                    return ap if dt == F32R else ap.bitcast(F32)

                pe.wait_ge(ffn_in, 48)
                for b, cc, c in chunks(pe):
                    def gate_up(i):
                        n = IT * c + i
                        if i >= 2:
                            pe.wait_ge(hid_ready, n - 1)
                        cols = slice(i * P, (i + 1) * P)
                        for k, (w, done) in enumerate(((wg_sb, g_ps), (wu_sb, u_ps))):
                            product(ps[:, T_BANK + 2 * (i % 2) + k, :],
                                    [(t(w[:, kc, cols]), t(xT[:, kc, :])) for kc in range(KC) for xT in (xT_hi, xT_lo)]).then_inc(done, 1)

                    def down(i):
                        if i == 0:
                            pe.wait_ge(x2_ready, TJ * N_CH)
                            pe.wait_ge(y_scaled, TJ * c)
                        pe.wait_ge(hid_hi_done, IT * c + i + 1)
                        pe.wait_ge(hid_lo_done, IT * c + i + 1)
                        for j in range(TJ):
                            tile = slice(j * P, (j + 1) * P)
                            for k, h in enumerate((hid_hi, hid_lo)):
                                ins = pe.matmul(ps[:, MM_BANK + j, :], t(h[:, i % 3, tile]), t(wd_sb[:, i, :]),
                                                start=(i == 0 and k == 0), stop=(i == IT - 1 and k == 1))
                        ins.then_inc(down_ps, 1)

                    def transpose_tiles(chunk, tiles):
                        for j in tiles:
                            pe.wait_ge(x2_tokens, TJ * chunk + j + 1)
                            transpose_tile(j, xst_c[:, j, :], TJ * (2 * N_CH + chunk), c2=True)

                    if cc == 0:
                        pe.wait_ge(hid_ready, IT * c)
                        transpose_tiles(c, range(TJ))
                    pe.wait_ge(t_lo, TJ * (2 * N_CH + c + 1))
                    gate_up(0)
                    for i in range(1, IT):
                        gate_up(i)
                        if cc == 0 and i == IT - 1:
                            pe.wait_ge(hid_ready, IT * c + IT - 1)
                            transpose_tiles(c + 1, range(0, 2))
                        down(i - 1)
                    if cc == 0:
                        pe.wait_ge(hid_ready, IT * (c + 1))
                        transpose_tiles(c + 1, range(2, TJ))
                    down(IT - 1)

            pe.wait_ge(flag_ready, 2)
            inexact = pe.value_load(flag_int[0:1, 0:1])
            with pe.If(inexact == 0):
                ffn_products(F32R)
            with pe.Else():
                ffn_products(F32)


def kernel(L0_attn_x, L0_attn_Wq, L0_attn_bq, L0_attn_Wk, L0_attn_bk, L0_attn_Wv, L0_attn_bv, L0_attn_Wo, L0_attn_bo,
           L0_ffn_gate_w, L0_ffn_up_w, L0_ffn_down_w, L0_ffn_gate_s, L0_ffn_up_s, L0_ffn_down_s):
    import numpy as np
    import concourse.bacc as bacc
    from concourse.bass_utils import run_bass_kernel_spmd

    def rows_on_partitions(w):
        return np.ascontiguousarray(np.asarray(w).reshape(-1, P, w.shape[1]).transpose(1, 0, 2).reshape(P, -1))

    order = np.arange(H).reshape(2, HALF, D // 2, 2).transpose(0, 3, 1, 2).reshape(-1)

    def per_partition(v, n):
        return np.ascontiguousarray(np.asarray(v).reshape(n, P).T)

    inv_freq = (1.0 / np.float32(10000.0) ** (np.arange(D // 2, dtype=np.float32) / np.float32(D // 2))).astype(np.float32)
    freqs = np.arange(S, dtype=np.float32)[None, :] * inv_freq[:, None]
    wq, wk = np.asarray(L0_attn_Wq), np.asarray(L0_attn_Wk)
    arrays = {
        "x": np.ascontiguousarray(L0_attn_x),
        "wq": rows_on_partitions(wq[order].T), "wk": rows_on_partitions(wk[order].T),
        "wv": rows_on_partitions(np.asarray(L0_attn_Wv).T), "wo": rows_on_partitions(np.asarray(L0_attn_Wo).T),
        "bqk": np.concatenate([per_partition(np.asarray(v)[order], KC) for v in (L0_attn_bq, L0_attn_bk)], axis=1),
        "bv": np.ascontiguousarray(L0_attn_bv), "bo": np.ascontiguousarray(L0_attn_bo),
        "ffn": np.concatenate([rows_on_partitions(np.asarray(w).T) for w in (L0_ffn_gate_w, L0_ffn_up_w, L0_ffn_down_w)], axis=1),
        "gs": per_partition(L0_ffn_gate_s, IT), "us": per_partition(L0_ffn_up_s, IT), "ds": np.ascontiguousarray(L0_ffn_down_s),
        "cos": np.tile(np.cos(freqs).astype(np.float32), (HALF, 1)), "sin": np.tile(np.sin(freqs).astype(np.float32), (HALF, 1)),
    }
    nc = bacc.Bacc("TRN2", target_bir_lowering=False, num_devices=1)
    aps = {k: nc.dram_tensor(f"in_{k}", v.shape, mybir.dt.from_np(v.dtype), kind="ExternalInput").ap() for k, v in arrays.items()}
    out = nc.dram_tensor("out", (NB, S, H), F32, kind="ExternalOutput").ap()
    transformer_block(nc, out=out, **aps)
    r = run_bass_kernel_spmd(nc, [{f"in_{k}": v for k, v in arrays.items()}], core_ids=[0])
    return r.results[0]["out"]
```

```python
from contextlib import ExitStack

import concourse.bass as bass
from concourse import mybir

ALU = mybir.AluOpType
ACT = mybir.ActivationFunctionType
AX_X = mybir.AxisListType.X
F32 = mybir.dt.float32
F32R = mybir.dt.float32r
F16 = mybir.dt.float16
BF16 = mybir.dt.bfloat16
I32 = mybir.dt.int32

P = 128
NB, S, H = 2, 1024, 512
NH, D = 16, 32
INTER = 1408
KC = H // P
IT = INTER // P
CH = 512
CC = S // CH
TJ = CH // P
KT = S // P
HEADS = NB * NH
HALF = P // (D // 2)
VW = 3 * D + 1
VP = VW + 1
SCALE = float(1.0 / (D ** 0.5))
LN_EPS = 1e-5
NEG = -1e30
SHIFT = 55.0
SLOTS = 4
K_DOT = 3 * D
K_ALL = K_DOT + 3

S_PIECES = []
for qt in range(KT):
    need = P * (qt + 1)
    if need <= 512:
        S_PIECES.append((qt, 0, max(need, 256), 0))
    else:
        first = 384 if need == 640 else 512
        S_PIECES += [(qt, 0, first, 0), (qt, first, need - first, 1)]
S_PIECES.sort(key=lambda piece: (-piece[2], -piece[0]))
M_ENTRY = 5
M_AFTER = 4
S_BANKS = [[piece] for piece in S_PIECES[:-2]] + [S_PIECES[-2:]]
S_BANKS.insert(M_ENTRY, [])
ST_PIECES = [(0, 0, 512, 0), (0, 512, 512, 512), (1, 128, 384, 128), (1, 512, 512, 512),
             (2, 256, 384, 256), (2, 640, 384, 640), (7, 768, 256, 896), (3, 384, 384, 384), (3, 768, 256, 768),
             (6, 768, 256, 768), (4, 512, 512, 512), (5, 640, 384, 640)]
KT_ORDER = list(dict.fromkeys(p[0] for p in ST_PIECES))
NPC = len(ST_PIECES)
NS = NPC - 1
assert len(S_BANKS) == NPC


def s_before(entry):
    return entry - (entry > M_ENTRY)


LAST_PIECE = [max(i for i, p in enumerate(ST_PIECES) if p[0] == kt) for kt in range(KT)]
P_OFF = [sum(S - P * k for k in range(kt)) for kt in range(KT + 1)]
PV_TERMS = [(kt, qt, part) for kt in KT_ORDER for qt in range(kt, KT) for part in range(2)]
PV_TERMS.sort(key=lambda term: (KT_ORDER.index(term[0]) // 2, term[1] >= KT // 2))
LAST_KEYS = [[kt for kt in KT_ORDER if kt <= qt][-1] for qt in range(KT)]
PV_LAST_FIRST = [term for term in PV_TERMS if term[1] < KT // 2][-1]
PV_COUNTS = [4, 9, 6, 8, 7, 9, 5, 8, 3, 2, 3, 8]
assert len(PV_COUNTS) == NPC and sum(PV_COUNTS) == len(PV_TERMS)
def splitting(vector):
    return {"high": list(vector), "low": list(vector), "pool": [kt for kt in KT_ORDER if kt not in vector]}


LAST_OWN = (1, 3)
SPLIT = splitting((7, 5))
SPLIT_LAST = splitting(LAST_OWN + (7, 5))
LAST_HEADS = HEADS - 2


def split_of(r):
    return SPLIT_LAST if type(r) is int and r >= LAST_HEADS else SPLIT


def split_count(which, r, kt):
    if split_of(r) is SPLIT:
        return len(SPLIT[which]) * r + SPLIT[which].index(kt) + 1
    return len(SPLIT[which]) * LAST_HEADS + len(SPLIT_LAST[which]) * (r - LAST_HEADS) + SPLIT_LAST[which].index(kt) + 1


FFN_COLS = KC * INTER
W_PIECE = 2 * H
FLAG_W = 768
FLAG_N = 3 * FFN_COLS // FLAG_W
FLAG_CH = -(-FLAG_N // (NB * CC))
FLAG_LAST = FLAG_N - (NB * CC - 1) * FLAG_CH
FLAG_BESIDE = range(FLAG_LAST - 1, FLAG_LAST)
assert FLAG_N * FLAG_W == 3 * FFN_COLS and FLAG_LAST >= 3
FFN_PIECE = 3 * FFN_COLS // HEADS
assert IT * H == FFN_COLS


def transformer_block(nc, x, wq, wk, wv, wo, bqk, bv, bo, ffn, gs, us, ds, cos, sin, shift_rows, out):
    ctx = ExitStack()
    with ctx:
        def sb(name, shape, dt, scope=ctx):
            return scope.enter_context(nc.sbuf_tensor(name, shape, dt))

        def sem(name):
            return ctx.enter_context(nc.semaphore(name))

        scratch = nc.dram_tensor("qk_scratch", [2, 4, HEADS, D // 2, S], F32, kind="Internal").ap()
        shift_copy = nc.dram_tensor("shift_copy", [1 + K_ALL - K_DOT, SLOTS * S], F32, kind="Internal").ap()
        ffn_copy = nc.dram_tensor("ffn_copy", [P, 3 * FFN_COLS], F32, kind="Internal").ap()

        with ExitStack() as under_xT:
            masked = sb("masked", [P, 2, 512], BF16, under_xT)
        xT_hi = sb("xT_hi", [P, KC, CH], F32R)
        xT_lo = sb("xT_lo", [P, KC, CH], F32R)
        ident = sb("ident", [P, P], F32)
        ident_b = sb("ident_b", [P, P], BF16)
        mask_kq = sb("mask_kq", [P, P], BF16)
        mask_qk = sb("mask_qk", [P, 512], BF16)
        stats = sb("stats", [P, TJ, 6], F32)
        moments = sb("moments", [P, TJ, 2], F32)
        std = sb("std", [P, TJ], F32)
        rstd = sb("rstd", [P, TJ], F32)
        eps = sb("eps", [P, 1], F32)
        bqk_sb = sb("bqk_sb", [P, 8], F32)
        gs_sb = sb("gs_sb", [P, IT], F32)
        us_sb = sb("us_sb", [P, IT], F32)
        flag_bits = sb("flag_bits", [P, FLAG_W], I32)
        flag_part = sb("flag_part", [P, 1], F32)
        flag_all = sb("flag_all", [P, 1], F32)
        flag_int = sb("flag_int", [P, 1], I32)
        row_max = sb("row_max", [P, 2, KT, 2], F32)
        max8 = sb("max8", [P, KT], F32)
        neg_max = sb("neg_max", [P, 2 * KT], F32R)
        neg_max_T = sb("neg_max_T", [2 * KT, 2, P], F32)
        with ExitStack() as under_tok:
            rot = sb("rot", [P, 2, 2, CH], F32, under_tok)
            st_hi = sb("st_hi", [P, 2, 2, CH], F32R, under_tok)
            st_lo = sb("st_lo", [P, 2, 2, CH], F32R, under_tok)
            with ExitStack() as under_wo_st:
                even = sb("even", [P, 2, CH], F32, under_wo_st)
                odd = sb("odd", [P, 2, CH], F32, under_wo_st)
            wo_st = sb("wo_st", [P, KC, H], F32, under_tok)
        tok = sb("tok", [P, KT, NB, H], F32)
        with ExitStack() as under_wo:
            w_st = sb("w_st", [P, 2, W_PIECE], F32, under_wo)
            cos_sb = sb("cos_sb", [P, S], F32, under_wo)
            sin_sb = sb("sin_sb", [P, S], F32, under_wo)
        wo_lo = sb("wo_lo", [P, KC, H], F32R)
        wo_hi = sb("wo_hi", [P, KC, H], F32R)
        with ExitStack() as stage_ab:
            v_sb = sb("v_sb", [P, KT, HEADS, VP], BF16, stage_ab)
            with ExitStack() as stage_a:
                w_split = [[sb(f"w_{part}{m}", [P, KC, H], F32R, stage_a) for part in ("hi", "lo")] for m in range(3)]
                w_hi, w_lo = [w[0] for w in w_split], [w[1] for w in w_split]
                x_st = sb("x_st", [P, TJ, H], F32, stage_a)
                xn = sb("xn", [P, TJ, H], F32, stage_a)
                bv_sb = sb("bv_sb", [P, H], F32, stage_a)
                osin = sb("osin", [P, CH], F32, stage_a)
                ocos = sb("ocos", [P, 2, CH], F32, stage_a)
                esin = sb("esin", [P, 2, CH], F32, stage_a)
                v32 = sb("v32", [P, TJ, H], F32, stage_a)
                v_rest = sb("v_rest", [P, 2, H], F32, stage_a)
            with ExitStack() as stage_b:
                q_st = sb("q_st", [P, SLOTS, S], F32R, stage_b)
                k_st = sb("k_st", [P, SLOTS, S], F32R, stage_b)
                p32 = sb("p32", [P, P_OFF[KT]], F32, stage_b)
                p_hi = sb("p_hi", [P, 2, P_OFF[KT]], F16, stage_b)
                p_lo = sb("p_lo", [P, 2, P_OFF[KT]], F16, stage_b)
                o_sum = sb("o_sum", [P, KT, D], F32, stage_b)
                o_rec = sb("o_rec", [P, KT], F32, stage_b)
        wg_sb = sb("wg_sb", [P, KC, INTER], F32R)
        wu_sb = sb("wu_sb", [P, KC, INTER], F32R)
        wd_sb = sb("wd_sb", [P, IT, H], F32R)
        xh = sb("xh", [P, KT, NB, H], F32)
        xst_c = sb("xst_c", [P, TJ, H], F32)
        ds_sb = sb("ds_sb", [P, H], F32)
        with ExitStack() as stage_c1:
            xr = sb("xr", [P, CC, TJ, H], F32, stage_c1)
            bo_sb = sb("bo_sb", [P, H], F32, stage_c1)
        with ExitStack() as stage_c2:
            silu = sb("silu", [P, 2, CH], F32, stage_c2)
            hid = sb("hid", [P, 2, CH], F32, stage_c2)
            hid_hi = sb("hid_hi", [P, 3, CH], F32R, stage_c2)
            hid_lo = sb("hid_lo", [P, 3, CH], F32R, stage_c2)
            y_sb = sb("y_sb", [P, TJ, H], F32, stage_c2)

        ps = ctx.enter_context(nc.psum_tensor("ps", [P, 8, 512], F32))
        T_BANK, MM_BANK = 0, 4
        S_BANK, ST_BANK, O_BANK = 0, 3, 6
        RING = 3
        M_BANK = S_BANK + M_ENTRY % RING

        x_tile = [sem(f"x_tile{j}") for j in range(TJ)]
        x_in = sem("x_in")
        const_in = sem("const_in")
        w_in = [sem(f"w_in{k}") for k in range(2)]
        ffn_copied = sem("ffn_copied")
        consts = sem("consts")
        w_hi_done = sem("w_hi_done")
        w_lo_done = sem("w_lo_done")
        flag_init = sem("flag_init")
        flag_done = sem("flag_done")
        sqrt_loaded = sem("sqrt_loaded")
        exp_loaded = sem("exp_loaded")
        ln_stats = sem("ln_stats")
        ln_moments = sem("ln_moments")
        ln_std = sem("ln_std")
        ln_rstd = sem("ln_rstd")
        ln_done = sem("ln_done")
        x2_tokens = sem("x2_tokens")
        t_ps = sem("t_ps")
        t_hi = sem("t_hi")
        t_lo = sem("t_lo")
        qk_ps = sem("qk_ps")
        eo_ready = sem("eo_ready")
        rope_prod = sem("rope_prod")
        pool_prod = sem("pool_prod")
        rope_done = sem("rope_done")
        rot_hi = sem("rot_hi")
        rot_lo = sem("rot_lo")
        scr_out = [sem(f"scr_out{k}") for k in range(2)]
        v_ps = sem("v_ps")
        v32_ready = sem("v32_ready")
        v1_ready = sem("v1_ready")
        rest_ready = sem("rest_ready")
        v2_ready = sem("v2_ready")
        v3_ready = sem("v3_ready")
        shift_copied = sem("shift_copied")
        q_rows = sem("q_rows")
        k_rows = sem("k_rows")
        row_max_init = sem("row_max_init")
        head_in = [sem(f"head_in{k}") for k in range(SLOTS)]
        s_ps = sem("s_ps")
        s_max = sem("s_max")
        max_step = sem("max_step")
        max_ready = sem("max_ready")
        max_T_ps = sem("max_T_ps")
        max_T = sem("max_T")
        max_in = [sem(f"max_in{k}") for k in range(SLOTS)]
        st_ps = sem("st_ps")
        exp_done = sem("exp_done")
        p_hi_dve = sem("p_hi_dve")
        p_lo_pool = sem("p_lo_pool")
        p_lo_dve = sem("p_lo_dve")
        pv_first = sem("pv_first")
        pv_done = sem("pv_done")
        o_sums = sem("o_sums")
        o_parts = sem("o_parts")
        o_done = sem("o_done")
        wo_in = sem("wo_in")
        wo_hi_done = sem("wo_hi_done")
        wo_lo_done = sem("wo_lo_done")
        c_in = sem("c_in")
        gate_in = sem("gate_in")
        up_in = sem("up_in")
        down_in = sem("down_in")
        xr_in = [sem(f"xr_in{k}") for k in range(NB * CC)]
        xr_ready = sem("xr_ready")
        o_ps = sem("o_ps")
        x2_ready = sem("x2_ready")
        flag_ready = sem("flag_ready")
        g_ps = sem("g_ps")
        u_ps = sem("u_ps")
        silu_ready = sem("silu_ready")
        hid_ready = sem("hid_ready")
        hid_hi_done = sem("hid_hi_done")
        hid_lo_done = sem("hid_lo_done")
        down_ps = sem("down_ps")
        y_scaled = sem("y_scaled")
        y_ps = sem("y_ps")
        y_ready = [sem(f"y_ready{j}") for j in range(TJ)]
        y_out = [sem(f"y_out{j}") for j in range(TJ)]

        N_CH = NB * CC
        block = ctx.enter_context(nc.Block())

        def stage_a_done(eng):
            eng.wait_ge(v32_ready, N_CH * TJ)
            eng.wait_ge(v2_ready, N_CH * TJ)
            eng.wait_ge(v3_ready, N_CH * TJ)
            eng.wait_ge(v_ps, N_CH * TJ)
            for k in range(2):
                eng.wait_ge(scr_out[k], 32 * 2 * N_CH)

        def stage_b_done(eng):
            eng.wait_ge(pv_done, HEADS)
            eng.wait_ge(o_done, HEADS)
            eng.wait_ge(st_ps, NPC * HEADS)
            eng.wait_ge(s_max, NS * HEADS)
            eng.wait_ge(max_T, HEADS)

        def stage_c1_done(eng):
            eng.wait_ge(x2_ready, N_CH * TJ)

        def chunks(eng):
            with eng.Fori(0, NB) as b:
                for cc in range(CC):
                    yield b, cc, b * CC + cc

        def t_bank(j, c2=False):
            return T_BANK + ((j + 2) % TJ if c2 else j)

        @block.sync
        def _(sp):
            def load_x(dst, c):
                b, cc = divmod(c, CC)
                return sp.dma_start(dst, x[b, cc * CH:(cc + 1) * CH, :].rearrange("(j p) h -> p j h", p=P))

            for j in range(TJ):
                sp.dma_start(x_st[:, j, :], x[0, j * P:(j + 1) * P, :]).then_inc(x_tile[j], 16)
            for n in range(6):
                if n >= 2:
                    sp.wait_ge(w_lo_done, n - 1)
                src = (wq, wk, wv)[n // 2][:, n % 2 * W_PIECE:(n % 2 + 1) * W_PIECE]
                sp.dma_start(w_st[:, n % 2, :], src).then_inc(w_in[n % 2], 16)
                if n == 1:
                    sp.dma_start(bqk_sb[:, :], bqk).then_inc(const_in, 16)
                    sp.dma_start(cos_sb[:, :], cos).then_inc(const_in, 16)
                    sp.dma_start(sin_sb[:, :], sin).then_inc(const_in, 16)
                    sp.dma_start(bv_sb[:, :], bv.partition_broadcast(P)).then_inc(const_in, 16)
                    sp.dma_start(gs_sb[:, :], gs).then_inc(const_in, 16)
                    sp.dma_start(us_sb[:, :], us).then_inc(const_in, 16)
                if n == 2:
                    sp.wait_ge(ln_done, 1)
                    load_x(x_st[:, :, :], 1).then_inc(x_in, 16)

            def load_flag_piece(c, k):
                sp.wait_ge(flag_done, FLAG_CH * c + max(k - 1, 0))
                sp.dma_start(w_st[:, k % 2, 0:FLAG_W], ffn[:, bass.ds((FLAG_CH * c + k) * FLAG_W, FLAG_W)]).then_inc(w_in[k % 2], 16)

            def load_head(t, slot):
                q, k = scratch[0], scratch[1]
                at = bass.ds(t, 1)
                hi, both = slice(0, 2), slice(0, 4)
                for dst, rows, src, parts in ((q_st, slice(0, 32), q, hi), (q_st, slice(32, 96), q, both),
                                              (k_st, slice(0, 64), k, both), (k_st, slice(64, 96), k, hi)):
                    sp.dma_start(dst[rows, slot, :].bitcast(F32), src[parts, at, :, :].rearrange("r o i s -> r (o i) s")).then_inc(head_in[slot], 16)

            sp.dma_start(shift_copy, shift_rows).then_inc(shift_copied, 16)
            sp.wait_ge(w_lo_done, 6)
            for c in range(N_CH):
                b, cc = divmod(c, CC)
                if 2 <= c + 1 < N_CH:
                    sp.wait_ge(ln_done, c + 1)
                    load_x(x_st[:, :, :], c + 1).then_inc(x_in, 16)
                load_flag_piece(c, 0)
                load_flag_piece(c, 1)
                for p in range(4):
                    if c == N_CH - 1 and p == 2:
                        sp.wait_ge(qk_ps, 4 * N_CH)
                        for k in range(2):
                            sp.wait_ge(scr_out[k], 32 * 2 * CC)
                        sp.wait_ge(shift_copied, 16)
                        sp.dma_start(q_st[K_DOT + 2:K_ALL, :, :].rearrange("p t s -> p (t s)").bitcast(F32), shift_copy[0:1, :]).then_inc(q_rows, 16)
                        sp.dma_start(k_st[K_DOT:K_ALL, :, :].rearrange("p t s -> p (t s)").bitcast(F32), shift_copy[1:, :]).then_inc(k_rows, 16)
                        for t in range(2):
                            load_head(t, t)
                    for half, done, st in ((0, rot_hi, st_hi), (1, rot_lo, st_lo)):
                        sp.wait_ge(done, 4 * c + p + 1)
                        dst = scratch[p // 2, 2 * half:2 * half + 2, b * NH + p % 2 * HALF:b * NH + (p % 2 + 1) * HALF, :, cc * CH:(cc + 1) * CH]
                        sp.dma_start(dst.rearrange("e h i s -> (h i) e s"), st[:, p % 2, :, :].bitcast(F32)).then_inc(scr_out[p % 2], 16)
                    for k in ((), (2,), (3,) if c < N_CH - 1 else (), (4, 5) if c < N_CH - 1 else ())[p]:
                        load_flag_piece(c, k)

            load_head(2, 2)
            sp.wait_ge(rope_done, 4 * N_CH)
            sp.dma_start(wo_st[:, :, :], wo).then_inc(wo_in, 16)

            def load_max(u, slot):
                sp.wait_ge(max_T, u + 1)
                for part in range(2):
                    sp.dma_start(q_st[K_DOT + part:K_DOT + part + 1, slot, :].bitcast(F32), neg_max_T[part * KT:(part + 1) * KT, slot % 2, :]).then_inc(max_in[slot], 16)

            def b_step(t, j, last=False):
                if not (last and j >= SLOTS - 1):
                    load_max(t + 1, (j + 1) % SLOTS)
                cols = bass.ds(t * FFN_PIECE, FFN_PIECE)
                sp.dma_start(ffn_copy[:, cols], ffn[:, cols]).then_inc(ffn_copied, 16)
                if not last:
                    sp.wait_ge(st_ps, NPC * (t + 1))
                    load_head(t + SLOTS, j)

            stage_a_done(sp)
            load_max(0, 0)
            load_head(3, 3)
            for k in FLAG_BESIDE:
                load_flag_piece(N_CH - 1, k)
            for t in range(SLOTS):
                b_step(t, t)
            with sp.Fori(1, HEADS // SLOTS - 1) as it:
                for j in range(SLOTS):
                    b_step(it * SLOTS + j, j)
            for j in range(SLOTS):
                b_step(HEADS - SLOTS + j, j, last=True)

            stage_b_done(sp)
            sp.dma_start(bo_sb[:, :], bo.partition_broadcast(P)).then_inc(c_in, 16)
            sp.dma_start(ds_sb[:, :], ds.partition_broadcast(P)).then_inc(c_in, 16)
            load_x(xr[:, 0, :, :], 0).then_inc(xr_in[0], 16)
            load_x(xr[:, 1, :, :], 1).then_inc(xr_in[1], 16)
            sp.wait_ge(ffn_copied, 16 * HEADS)
            for m, (dst, done) in enumerate(((wg_sb, gate_in), (wu_sb, up_in), (wd_sb, down_in))):
                sp.dma_start(dst[:, :, :].rearrange("p a n -> p (a n)").bitcast(F32), ffn_copy[:, m * FFN_COLS:(m + 1) * FFN_COLS]).then_inc(done, 16)
                if m < CC:
                    sp.wait_ge(x2_ready, TJ * (m + 1))
                    load_x(xr[:, m, :, :], CC + m).then_inc(xr_in[CC + m], 16)
            for b, cc, c in chunks(sp):
                for j in range(TJ):
                    sp.wait_ge(y_ready[j], c + 1)
                    sp.dma_start(out[bass.ds(b, 1), cc * CH + j * P:cc * CH + (j + 1) * P, :].rearrange("o p h -> (o p) h"), y_sb[:, j, :]).then_inc(y_out[j], 16)
            for j in range(TJ):
                sp.wait_ge(y_out[j], 16 * N_CH)

        @block.gpsimd
        def _(pool):
            pool.memset(ident[:, :], 0.0)
            pool.memset(ident_b[:, :], 0.0)
            pool.memset(mask_kq[:, :], 0.0)
            pool.memset(mask_qk[:, :], 0.0)
            pool.memset(eps[:, :], LN_EPS)
            pool.memset(v_sb[:, :, :, 3 * D:VP], 1.0).then_inc(consts, 1)
            pool.wait_ge(consts, 1)
            for m in (ident, ident_b):
                pool.affine_select(out=m[:, :], in_=m[:, :], compare_op=ALU.not_equal, fill=1.0, base=0,
                                   pattern=[[-1, P]], channel_multiplier=1)
            pool.affine_select(out=mask_kq[:, :], in_=mask_kq[:, :], compare_op=ALU.is_ge, fill=NEG, base=0,
                               pattern=[[1, P]], channel_multiplier=-1)
            pool.affine_select(out=mask_qk[:, :], in_=mask_qk[:, :], compare_op=ALU.is_ge, fill=NEG, base=512 - P,
                               pattern=[[-1, 512]], channel_multiplier=1).then_inc(consts, 1)
            pool.wait_ge(const_in, 96)

            for b, cc, c in chunks(pool):
                pos = slice(cc * CH, (cc + 1) * CH)
                for p in range(4):
                    n = 4 * c + p
                    pool.wait_ge(eo_ready, n + 1)
                    pool.wait_ge(rope_done, 4 * c + max(p - 1, 0))
                    pool.tensor_tensor(ocos[:, p % 2, :], odd[:, p % 2, :], cos_sb[:, pos], ALU.mult)
                    pool.tensor_tensor(esin[:, p % 2, :], even[:, p % 2, :], sin_sb[:, pos], ALU.mult).then_inc(pool_prod, 1)

                def rest(j):
                    pool.wait_ge(v1_ready, TJ * c + j + 1)
                    pool.wait_ge(v2_ready, TJ * c + max(j - 1, 0))
                    pool.wait_ge(v3_ready, TJ * c + max(j - 1, 0))
                    v1 = v_sb[:, cc * TJ + j, bass.ds(b * NH, NH), 0:D]
                    pool.tensor_tensor(v_rest[:, j % 2, :].rearrange("p (h d) -> p h d", d=D),
                                       v32[:, j, :].rearrange("p (h d) -> p h d", d=D), v1, ALU.subtract).then_inc(rest_ready, 1)

                def third(j):
                    pool.wait_ge(v2_ready, TJ * c + j + 1)
                    v2 = v_sb[:, cc * TJ + j, bass.ds(b * NH, NH), D:2 * D]
                    v3 = v_sb[:, cc * TJ + j, bass.ds(b * NH, NH), 2 * D:3 * D]
                    pool.tensor_tensor(v3, v_rest[:, j % 2, :].rearrange("p (h d) -> p h d", d=D), v2, ALU.subtract).then_inc(v3_ready, 1)

                rest(0)
                rest(1)
                third(0)
                rest(2)
                third(1)
                rest(3)
                third(2)
                third(3)

            stage_a_done(pool)

            def b_step(t, j):
                for kt in split_of(t)["pool"]:
                    pool.wait_ge(exp_done, NPC * t + LAST_PIECE[kt] + 1)
                    cols = slice(P_OFF[kt], P_OFF[kt + 1])
                    pool.tensor_tensor(p_lo[:, j % 2, cols], p32[:, cols], p_hi[:, j % 2, cols], ALU.subtract).then_inc(p_lo_pool, 1)

            with pool.Fori(0, HEADS // SLOTS - 1) as it:
                for j in range(SLOTS):
                    b_step(it * SLOTS + j, j)
            for j in range(SLOTS):
                b_step(HEADS - SLOTS + j, j)

            stage_b_done(pool)
            pool.wait_ge(c_in, 32)
            for c in range(N_CH):
                pool.wait_ge(xr_in[c], 16)
                for j in range(TJ):
                    xt = xr[:, c % CC, j, :]
                    pool.tensor_tensor(xt, xt, bo_sb[:, :], ALU.add).then_inc(xr_ready, 1)
                if c == 0:
                    pool.wait_ge(flag_done, FLAG_N + 1)
                    pool.partition_all_reduce(flag_all[:, :], flag_part[:, :], P, bass.bass_isa.ReduceOp.max).then_inc(flag_ready, 1)
                    pool.wait_ge(flag_ready, 1)
                    pool.tensor_copy(flag_int[:, :], flag_all[:, :]).then_inc(flag_ready, 1)

            stage_c1_done(pool)
            for b, cc, c in chunks(pool):
                for i in range(IT):
                    pool.wait_ge(hid_hi_done, IT * c + i + 1)
                    pool.wait_ge(down_ps, IT * c + max(i - 2, 0))
                    pool.tensor_tensor(hid_lo[:, i % 3, :], hid[:, i % 2, :], hid_hi[:, i % 3, :].bitcast(F32), ALU.subtract).then_inc(hid_lo_done, 1)
                for j in range(0, TJ, 2):
                    pool.wait_ge(y_scaled, TJ * c + j + 1)
                    pool.tensor_tensor(y_sb[:, j, :], y_sb[:, j, :], tok[:, cc * TJ + j, bass.ds(b, 1), :].rearrange("p o h -> p (o h)"), ALU.add).then_inc(y_ready[j], 1)

        @block.scalar
        def _(act):
            def std_of(n):
                act.wait_ge(ln_moments, n + 1)
                act.activation(std[:, :], moments[:, :, 1], ACT.Sqrt, bias=eps[:, 0:1]).then_inc(ln_std, 1)

            def transposed_hi(n, j, c2=False):
                act.wait_ge(t_ps, TJ * n + j + 1)
                act.copy(xT_hi[:, :, j * P:(j + 1) * P], ps[:, t_bank(j, c2), :].rearrange("p (k t) -> p k t", t=P)).then_inc(t_hi, 1)

            act.wait_ge(consts, 2)
            act.activation(std[:, 0:1], eps[:, 0:1], ACT.Sqrt).then_inc(sqrt_loaded, 1)
            act.wait_ge(sqrt_loaded, 1)
            std_of(0)

            def weight_hi(n):
                m, cols = n // 2, slice(n % 2 * 2, n % 2 * 2 + 2)
                act.wait_ge(w_in[n % 2], 16 * (n // 2 + 1))
                act.copy(w_hi[m][:, cols, :].rearrange("p a n -> p (a n)"), w_st[:, n % 2, :]).then_inc(w_hi_done, 1)

            weight_hi(0)
            transposed_hi(0, 0)
            transposed_hi(0, 1)
            weight_hi(1)
            transposed_hi(0, 2)
            transposed_hi(0, 3)
            weight_hi(2)
            weight_hi(3)
            std_of(1)
            act.wait_ge(const_in, 96)
            for c in range(N_CH):
                b, cc = divmod(c, CC)

                def evacuate(p):
                    n = 4 * c + p
                    act.wait_ge(qk_ps, n + 1)
                    if n >= 2:
                        act.wait_ge(rope_done, n - 1)
                    bank = MM_BANK + 2 * (p % 2)
                    act.activation(even[:, p % 2, :], ps[:, bank, :], ACT.Identity, bias=bqk_sb[:, 2 * p:2 * p + 1])
                    act.activation(odd[:, p % 2, :], ps[:, bank + 1, :], ACT.Identity, bias=bqk_sb[:, 2 * p + 1:2 * p + 2]).then_inc(eo_ready, 1)

                def high(p):
                    n = 4 * c + p
                    act.wait_ge(rope_done, n + 1)
                    if n >= 2:
                        act.wait_ge(scr_out[p % 2], 32 * (n // 2))
                    act.copy(st_hi[:, p % 2, :, :].rearrange("p e s -> p (e s)"),
                             rot[:, p % 2, :, :].rearrange("p e s -> p (e s)")).then_inc(rot_hi, 1)

                evacuate(0)
                if c == 0:
                    weight_hi(4)
                evacuate(1)
                high(0)
                if c == 0:
                    weight_hi(5)
                if 0 < c < N_CH - 1:
                    std_of(c + 1)
                evacuate(2)
                high(1)
                evacuate(3)
                high(2)
                if c == N_CH - 1:
                    high(3)

                def v_part(j, part, src, ready, done):
                    act.wait_ge(ready, TJ * c + j + 1)
                    act.copy(v_sb[:, cc * TJ + j, b * NH:(b + 1) * NH, part * D:(part + 1) * D],
                             src[:, j if part == 0 else j % 2, :].rearrange("p (h d) -> p h d", d=D)).then_inc(done, 1)

                def next_tile(j):
                    if c + 1 < N_CH:
                        act.wait_ge(v_ps, TJ * c + j + 1)
                        transposed_hi(c + 1, j)

                v_part(0, 0, v32, v32_ready, v1_ready)
                next_tile(0)
                v_part(1, 0, v32, v32_ready, v1_ready)
                next_tile(1)
                next_tile(2)
                next_tile(3)
                if c < N_CH - 1:
                    high(3)
                v_part(0, 1, v_rest, rest_ready, v2_ready)
                v_part(2, 0, v32, v32_ready, v1_ready)
                v_part(1, 1, v_rest, rest_ready, v2_ready)
                v_part(3, 0, v32, v32_ready, v1_ready)
                v_part(2, 1, v_rest, rest_ready, v2_ready)
                v_part(3, 1, v_rest, rest_ready, v2_ready)


            def exp_piece(t, j, i):
                kt, q0, w, keep = ST_PIECES[i]
                act.wait_ge(st_ps, NPC * t + i + 1)
                at = P_OFF[kt] + keep - P * kt
                scores = ps[:, ST_BANK + i % RING, keep - q0:w]
                ins = act.activation(p32[:, at:at + q0 + w - keep], scores, ACT.Exp, scale=SCALE)
                if kt not in split_of(t)["high"]:
                    ins = act.activation(p_hi[:, j % 2, at:at + q0 + w - keep], scores, ACT.Exp, scale=SCALE)
                ins.then_inc(exp_done, 1)

            def b_step(t, j, it, first=False, last=False):
                def next_max():
                    act.wait_ge(max_T_ps, t + 2)
                    if not (first and j < 1):
                        act.wait_ge(max_in[(j - 1) % SLOTS], 32 * (it + (j - 1) // SLOTS + 1))
                    act.copy(neg_max_T[:, (j + 1) % 2, :], ps[0:2 * KT, M_BANK, 0:P]).then_inc(max_T, 1)

                def exps(kt):
                    if not (first and j == 0):
                        if kt in split_of(t - 1)["pool"]:
                            act.wait_ge(p_lo_pool, split_count("pool", t - 1, kt))
                        else:
                            act.wait_ge(p_lo_dve, split_count("low", t - 1, kt))
                    for i in range(NPC):
                        if ST_PIECES[i][0] == kt:
                            exp_piece(t, j, i)
                            if i == M_AFTER and not (last and j == SLOTS - 1):
                                next_max()

                if not (first and j < 2):
                    act.wait_ge(pv_done, t - 1)
                for kt in KT_ORDER:
                    exps(kt)

            act.wait_ge(ln_rstd, N_CH)
            act.activation(std[:, 0:1], eps[:, 0:1], ACT.Exp).then_inc(exp_loaded, 1)
            act.wait_ge(exp_loaded, 1)
            act.wait_ge(max_T_ps, 1)
            act.copy(neg_max_T[:, 0, :], ps[0:2 * KT, M_BANK, 0:P]).then_inc(max_T, 1)
            act.wait_ge(rope_done, 4 * N_CH)
            act.wait_ge(wo_in, 16)
            act.copy(wo_hi[:, :, :], wo_st[:, :, :]).then_inc(wo_hi_done, 1)
            stage_a_done(act)
            for j in range(SLOTS):
                b_step(j, j, 0, first=True)
            with act.Fori(1, HEADS // SLOTS - 1) as it:
                for j in range(SLOTS):
                    b_step(it * SLOTS + j, j, it)
            for j in range(SLOTS):
                b_step(HEADS - SLOTS + j, j, HEADS // SLOTS - 1, last=True)

            act.wait_ge(s_max, NS * HEADS)
            for j in range(TJ):
                transposed_hi(N_CH, j)
            stage_b_done(act)

            def copy_tiles(c):
                b, cc = divmod(c, CC)
                act.wait_ge(ln_done, N_CH + c + 1)
                act.wait_ge(t_ps, TJ * (2 * N_CH + c))
                for j in range(TJ):
                    act.copy(xst_c[:, j, :], xh[:, cc * TJ + j, b, :]).then_inc(x2_tokens, 1)

            for c in range(N_CH):
                if c + 1 < N_CH:
                    for j in range(TJ):
                        act.wait_ge(o_ps, TJ * c + j + 1)
                        transposed_hi(N_CH + c + 1, j)
                else:
                    for j in range(TJ):
                        act.wait_ge(o_ps, TJ * c + j + 1)
                        transposed_hi(2 * N_CH, j, c2=True)
                if c == N_CH - 2:
                    copy_tiles(0)
                std_of(N_CH + c)

            stage_c1_done(act)
            for c in range(N_CH):
                for i in range(IT):
                    if i == 2 and c + 1 < N_CH:
                        copy_tiles(c + 1)
                    n = IT * c + i
                    act.wait_ge(g_ps, n + 1)
                    act.wait_ge(hid_ready, IT * c + max(i - 1, 0))
                    act.activation(silu[:, i % 2, :], ps[:, T_BANK + 2 * (i % 2), :], ACT.Silu, scale=gs_sb[:, i:i + 1]).then_inc(silu_ready, 1)
                    act.wait_ge(hid_ready, n + 1)
                    act.wait_ge(down_ps, IT * c + max(i - 2, 0))
                    act.copy(hid_hi[:, i % 3, :], hid[:, i % 2, :]).then_inc(hid_hi_done, 1)
                if c + 1 < N_CH:
                    for j in range(TJ):
                        transposed_hi(2 * N_CH + c + 1, j, c2=True)

        @block.vector
        def _(dve):
            def ln_first(n, tiles):
                for j in range(TJ):
                    ins = dve.bn_stats(stats[:, j, :], tiles[j])
                ins.then_inc(ln_stats, 1)
                ln_moments_of(n)

            def ln_moments_of(n):
                dve.wait_ge(ln_stats, n + 1)
                for j in range(TJ):
                    ins = dve.bn_aggr(moments[:, j, :], stats[:, j, :])
                ins.then_inc(ln_moments, 1)

            def ln_second(n, tiles, outs):
                dve.wait_ge(ln_std, n + 1)
                dve.reciprocal(rstd[:, :], std[:, :]).then_inc(ln_rstd, 1)
                dve.wait_ge(ln_rstd, n + 1)
                for j in range(TJ):
                    ins = dve.tensor_scalar(outs[j], tiles[j], moments[:, j, 0:1], rstd[:, j:j + 1], ALU.subtract, ALU.mult)
                ins.then_inc(ln_done, 1)

            def transposed_lo(n, j, c2=False):
                tile = slice(j * P, (j + 1) * P)
                dve.wait_ge(t_hi, TJ * n + j + 1)
                dve.tensor_tensor(xT_lo[:, :, tile], ps[:, t_bank(j, c2), :].rearrange("p (k t) -> p k t", t=P),
                                  xT_hi[:, :, tile].bitcast(F32), ALU.subtract).then_inc(t_lo, 1)

            x_tiles = [x_st[:, j, :] for j in range(TJ)]
            xn_tiles = [xn[:, j, :] for j in range(TJ)]

            def weight_lo(n):
                m, cols = n // 2, slice(n % 2 * 2, n % 2 * 2 + 2)
                dve.wait_ge(w_hi_done, n + 1)
                dve.tensor_tensor(w_lo[m][:, cols, :].rearrange("p a n -> p (a n)"), w_st[:, n % 2, :],
                                  w_hi[m][:, cols, :].rearrange("p a n -> p (a n)").bitcast(F32), ALU.subtract).then_inc(w_lo_done, 1)

            dve.memset(flag_bits[:, :], 0).then_inc(flag_init, 1)
            dve.wait_ge(flag_init, 1)
            for j in range(TJ):
                dve.wait_ge(x_tile[j], 16)
                ins = dve.bn_stats(stats[:, j, :], x_tiles[j])
            ins.then_inc(ln_stats, 1)
            ln_moments_of(0)
            ln_second(0, x_tiles, xn_tiles)
            weight_lo(0)
            transposed_lo(0, 0)
            transposed_lo(0, 1)
            weight_lo(1)
            transposed_lo(0, 2)
            transposed_lo(0, 3)
            weight_lo(2)
            weight_lo(3)
            dve.wait_ge(x_in, 16)
            ln_first(1, x_tiles)
            dve.wait_ge(const_in, 96)
            for c in range(N_CH):
                cc = c % CC
                pos = slice(cc * CH, (cc + 1) * CH)

                def rotate(p):
                    n = 4 * c + p
                    dve.wait_ge(eo_ready, n + 1)
                    if n >= 1:
                        dve.wait_ge(rope_done, n)
                    if n >= 2:
                        dve.wait_ge(rot_lo, n - 1)
                    dve.tensor_tensor(rot[:, p % 2, 0, :], even[:, p % 2, :], cos_sb[:, pos], ALU.mult)
                    dve.tensor_tensor(osin[:, :], odd[:, p % 2, :], sin_sb[:, pos], ALU.mult).then_inc(rope_prod, 1)
                    dve.wait_ge(rope_prod, n + 1)
                    dve.tensor_tensor(rot[:, p % 2, 0, :], rot[:, p % 2, 0, :], osin[:, :], ALU.subtract)
                    dve.wait_ge(pool_prod, n + 1)
                    dve.tensor_tensor(rot[:, p % 2, 1, :], ocos[:, p % 2, :], esin[:, p % 2, :], ALU.add).then_inc(rope_done, 1)

                def low(p):
                    n = 4 * c + p
                    dve.wait_ge(rot_hi, n + 1)
                    dve.tensor_tensor(st_lo[:, p % 2, :, :].rearrange("p e s -> p (e s)"), rot[:, p % 2, :, :].rearrange("p e s -> p (e s)"),
                                      st_hi[:, p % 2, :, :].rearrange("p e s -> p (e s)").bitcast(F32), ALU.subtract).then_inc(rot_lo, 1)

                def test_piece(k, c=c):
                    f = FLAG_CH * c + k
                    dve.wait_ge(w_in[k % 2], 16 * (3 + f // 2 + 1))
                    dve.wait_ge(flag_done, f)
                    dve.scalar_tensor_tensor(out=flag_bits[:, :], in0=w_st[:, k % 2, 0:FLAG_W].bitcast(I32), scalar=(1 << 12) - 1,
                                             in1=flag_bits[:, :], op0=ALU.bitwise_and, op1=ALU.bitwise_or).then_inc(flag_done, 1)

                def v_bias(j):
                    idx = TJ * c + j
                    dve.wait_ge(v_ps, idx + 1)
                    if c > 0:
                        dve.wait_ge(rest_ready, idx - TJ + 1)
                    dve.tensor_tensor(v32[:, j, :], ps[:, MM_BANK + j, :], bv_sb[:, :], ALU.add).then_inc(v32_ready, 1)

                def next_tile(j):
                    if c + 1 < N_CH:
                        transposed_lo(c + 1, j)

                rotate(0)
                if c == 0:
                    weight_lo(4)
                if 0 < c < N_CH - 1:
                    dve.wait_ge(x_in, 16 * (c + 1))
                    ln_first(c + 1, x_tiles)
                rotate(1)
                low(0)
                if c == 0:
                    weight_lo(5)
                if c + 1 < N_CH:
                    dve.wait_ge(t_ps, TJ * (c + 1))
                    ln_second(c + 1, x_tiles, xn_tiles)
                rotate(2)
                test_piece(0)
                low(1)
                test_piece(1)
                rotate(3)
                v_bias(0)
                low(2)
                test_piece(2)
                v_bias(1)
                if c + 1 < N_CH:
                    transposed_lo(c + 1, 0)
                    v_bias(2)
                    transposed_lo(c + 1, 1)
                    transposed_lo(c + 1, 2)
                    transposed_lo(c + 1, 3)
                else:
                    low(3)
                    v_bias(2)
                v_bias(3)
                if c + 1 < N_CH:
                    low(3)
                    test_piece(3)
                    test_piece(4)
                    test_piece(5)

            dve.memset(row_max[:, :, :, :], NEG).then_inc(row_max_init, 1)
            dve.wait_ge(row_max_init, 1)

            def max_piece(u, half, i, first=False):
                if i != M_ENTRY:
                    count = dve.compute_val(NS * u + s_before(i) + 1)
                    if not (first and i == 0):
                        two_before = dve.compute_val(NS * u + s_before(i) - 1)
                    dve.wait_ge(row_max_init, 1)
                    if not (first and i == 0):
                        dve.wait_ge(s_max, two_before)
                    dve.wait_ge(s_ps, count)
                    col = 0
                    for qt, k0, w, part in S_BANKS[i]:
                        kept = min(w, P * (qt + 1) - k0)
                        scores, dst = ps[:, S_BANK + i % RING, col:col + kept], row_max[:, half, qt, part:part + 1]
                        if k0 + w > P * qt:
                            ins = dve.tensor_tensor_reduce(masked[:, s_before(i) % 2, col:col + kept], scores, mask_qk[:, 512 - kept:512], 1.0, NEG, ALU.add, ALU.max, dst)
                        else:
                            ins = dve.tensor_reduce(dst, scores, AX_X, ALU.max)
                        col += w
                    ins.then_inc(s_max, 1)

            def negate_max(u, half, step):
                if step == 0:
                    dve.wait_ge(s_max, NS * (u + 1))
                    dve.tensor_reduce(max8[:, :], row_max[:, half, :, :], AX_X, ALU.max).then_inc(max_step, 1)
                elif step == 1:
                    dve.wait_ge(max_step, 2 * u + 1)
                    dve.wait_ge(max_T_ps, u)
                    dve.tensor_scalar(neg_max[:, 0:KT], max8[:, :], -1.0, None, ALU.mult).then_inc(max_step, 1)
                else:
                    dve.wait_ge(max_step, 2 * u + 2)
                    dve.scalar_tensor_tensor(out=neg_max[:, KT:2 * KT], in0=max8[:, :], scalar=-1.0, in1=neg_max[:, 0:KT].bitcast(F32),
                                             op0=ALU.mult, op1=ALU.subtract).then_inc(max_ready, 1)

            def high(r, half, kt):
                cols = slice(P_OFF[kt], P_OFF[kt + 1])
                dve.wait_ge(exp_done, NPC * r + LAST_PIECE[kt] + 1)
                dve.tensor_copy(p_hi[:, half, cols], p32[:, cols]).then_inc(p_hi_dve, 1)

            def low(r, half, kt):
                cols = slice(P_OFF[kt], P_OFF[kt + 1])
                if kt not in split_of(r)["high"]:
                    dve.wait_ge(exp_done, NPC * r + LAST_PIECE[kt] + 1)
                else:
                    dve.wait_ge(p_hi_dve, split_count("high", r, kt))
                dve.tensor_tensor(p_lo[:, half, cols], p32[:, cols], p_hi[:, half, cols], ALU.subtract).then_inc(p_lo_dve, 1)

            def output_parts(r, g):
                o = ps[:, O_BANK + g, 0:4 * VW].rearrange("p (q e) -> p q e", e=VW)
                q4 = slice(4 * g, 4 * g + 4)
                dve.wait_ge(o_done, r)
                dve.wait_ge(pv_first if g == 0 else pv_done, r + 1)
                dve.tensor_reduce(o_sum[:, q4, :], o[:, :, 0:3 * D].rearrange("p q (s d) -> p q d s", d=D), AX_X, ALU.add).then_inc(o_sums, 1)
                dve.reciprocal(o_rec[:, q4], o[:, :, 3 * D]).then_inc(o_parts, 1)

            def output(r):
                dve.wait_ge(o_parts, 2 * (r + 1))
                dst = tok[:, :, :, :].rearrange("p k b (h d) -> p k (b h) d", d=D)[:, :, bass.ds(r, 1), :].rearrange("p k o d -> p k (o d)")
                dve.tensor_tensor(dst, o_sum[:, :, :], o_rec[:, :].unsqueeze(2).broadcast_to([P, KT, D]), ALU.mult).then_inc(o_done, 1)

            SUMS_FIRST, SUMS_SECOND, OUTPUT = 10, 0, 1
            HIGH = {7: 1, 5: 4}
            LOW = {7: 2, 5: 7}
            assert sorted(HIGH, key=HIGH.get) == SPLIT["high"] and sorted(LOW, key=LOW.get) == SPLIT["low"]
            OWN = {1: 7, 3: 11}
            assert sorted(OWN) == sorted(LAST_OWN) and list(OWN) + SPLIT["low"] == SPLIT_LAST["low"] == SPLIT_LAST["high"]

            def beside(j, i):
                for k, at in zip(FLAG_BESIDE, ((0, 3),)):
                    if at == (j, i):
                        test_piece(k)
                for kc, at in enumerate(((0, 8), (0, 11), (1, 6), (1, 11))):
                    if at == (j, i):
                        dve.wait_ge(flag_done, FLAG_N)
                        dve.wait_ge(wo_hi_done, 1)
                        dve.tensor_tensor(wo_lo[:, kc, :], wo_st[:, kc, :], wo_hi[:, kc, :].bitcast(F32), ALU.subtract).then_inc(wo_lo_done, 1)

            def b_step(t, j, scores=True, negate=True, before=True, two_before=True, first=False, own=False):
                half = (j + 1) % 2
                for i in range(NPC):
                    if scores:
                        max_piece(t + 2, j % 2, i, first=not negate and not before)
                    if two_before and i == SUMS_SECOND:
                        output_parts(t - 2, 1)
                    if negate and i < 3:
                        negate_max(t + 1, half, i)
                    if two_before and i == OUTPUT:
                        output(t - 2)
                    if before:
                        for kt in KT_ORDER:
                            if HIGH.get(kt) == i:
                                high(t - 1, half, kt)
                            if LOW.get(kt) == i:
                                low(t - 1, half, kt)
                    if own:
                        for kt in OWN:
                            if OWN[kt] == i:
                                high(t, j % 2, kt)
                                low(t, j % 2, kt)
                    if before and i == SUMS_FIRST:
                        output_parts(t - 1, 0)
                    if first:
                        beside(j, i)

            b_step(-2, 0, negate=False, before=False, two_before=False)
            b_step(-1, 1, before=False, two_before=False)
            stage_a_done(dve)
            for j in range(SLOTS):
                if j == 2:
                    dve.wait_ge(wo_lo_done, KC)
                b_step(j, j, before=j > 0, two_before=j > 1, first=True)
            with dve.Fori(1, HEADS // SLOTS - 1) as it:
                for j in range(SLOTS):
                    b_step(it * SLOTS + j, j)
            for j in range(SLOTS + 1):
                t = HEADS - SLOTS + j
                b_step(t, j, scores=t + 2 < HEADS, negate=t + 1 < HEADS, own=LAST_HEADS <= t < HEADS)
            for j in range(TJ):
                transposed_lo(N_CH, j)
            output_parts(HEADS - 1, 1)
            output(HEADS - 1)

            stage_b_done(dve)

            def c_tiles(src, c):
                b, cc = divmod(c, CC)
                return [src[:, cc * TJ + j, b, :] for j in range(TJ)]

            dve.wait_ge(flag_done, FLAG_N)
            dve.tensor_reduce(flag_part[:, :], flag_bits[:, :], AX_X, ALU.max).then_inc(flag_done, 1)
            for c in range(N_CH):
                x2 = c_tiles(tok, c)
                for j in range(TJ):
                    dve.wait_ge(o_ps, TJ * c + j + 1)
                    dve.wait_ge(xr_ready, TJ * c + j + 1)
                    dve.tensor_tensor(x2[j], ps[:, MM_BANK + j, :], xr[:, c % CC, j, :], ALU.add).then_inc(x2_ready, 1)
                    transposed_lo(N_CH + c + 1, j, c2=(c == N_CH - 1))
                    if j == 1 and c > 0:
                        ln_second(N_CH + c - 1, c_tiles(tok, c - 1), c_tiles(xh, c - 1))
                    if j > 0:
                        dve.wait_ge(x2_ready, TJ * c + j)
                        dve.bn_stats(stats[:, j - 1, :], x2[j - 1])
                dve.wait_ge(x2_ready, TJ * (c + 1))
                dve.bn_stats(stats[:, TJ - 1, :], x2[TJ - 1]).then_inc(ln_stats, 1)
                ln_moments_of(N_CH + c)
            ln_second(2 * N_CH - 1, c_tiles(tok, N_CH - 1), c_tiles(xh, N_CH - 1))

            stage_c1_done(dve)
            dve.wait_ge(c_in, 32)
            for c in range(N_CH):
                for i in range(IT):
                    n = IT * c + i
                    dve.wait_ge(u_ps, n + 1)
                    dve.wait_ge(silu_ready, n + 1)
                    dve.wait_ge(hid_lo_done, IT * c + max(i - 1, 0))
                    dve.scalar_tensor_tensor(out=hid[:, i % 2, :], in0=ps[:, T_BANK + 2 * (i % 2) + 1, :], scalar=us_sb[:, i:i + 1],
                                             in1=silu[:, i % 2, :], op0=ALU.mult, op1=ALU.mult).then_inc(hid_ready, 1)
                if c + 1 < N_CH:
                    for j in range(TJ):
                        transposed_lo(2 * N_CH + c + 1, j, c2=True)

                def scale(j):
                    if j < TJ - 1:
                        dve.wait_ge(y_ps, (TJ - 1) * c + j + 1)
                    else:
                        dve.wait_ge(down_ps, IT * (c + 1))
                    dve.wait_ge(y_out[j], 16 * c)
                    dve.tensor_tensor(y_sb[:, j, :], ps[:, MM_BANK + j, :], ds_sb[:, :], ALU.mult).then_inc(y_scaled, 1)

                def add_x2(j):
                    dve.wait_ge(y_scaled, TJ * c + j + 1)
                    dve.tensor_tensor(y_sb[:, j, :], y_sb[:, j, :], c_tiles(tok, c)[j], ALU.add).then_inc(y_ready[j], 1)

                scale(0)
                scale(1)
                scale(2)
                add_x2(1)
                scale(3)
                add_x2(3)

        @block.tensor
        def _(pe):
            def transpose_tile(j, tokens, free=None, c2=False):
                if free is not None:
                    pe.wait_ge(t_lo, free)
                for kc in range(KC):
                    ins = pe.transpose(ps[:, t_bank(j, c2), kc * P:(kc + 1) * P], tokens[:, kc * P:(kc + 1) * P], ident[:, :])
                ins.then_inc(t_ps, 1)

            def product(dst, terms, low=None):
                for k, (w, m) in enumerate(terms):
                    if low is not None and k == 2 * KC:
                        pe.wait_ge(t_lo, low)
                    ins = pe.matmul(dst, w, m, start=(k == 0), stop=(k == len(terms) - 1))
                return ins

            THREE = ((0, xT_hi), (1, xT_hi), (0, xT_lo))
            pe.wait_ge(consts, 2)

            def a_chunk(c, first=False, last=False):
                pe.wait_ge(t_hi, TJ * (c + 1))
                for p in range(4):
                    pe.wait_ge(w_lo_done, 2 if p < 2 else 4)
                    if p < 2 and not first:
                        pe.wait_ge(v32_ready, TJ * c - 2 + 2 * p)
                    elif p >= 2:
                        pe.wait_ge(eo_ready, 4 * c + p - 1)
                    m, half = p // 2, p % 2
                    for eo in range(2):
                        cols = slice((2 * half + eo) * P, (2 * half + eo + 1) * P)
                        ins = product(ps[:, MM_BANK + 2 * half + eo, :],
                                      [(w_split[m][part][:, kc, cols], xT[:, kc, :]) for part, xT in THREE for kc in range(KC)],
                                      low=TJ * (c + 1) if p == 0 and eo == 0 else None)
                    ins.then_inc(qk_ps, 1)
                pe.wait_ge(w_lo_done, 6)
                for j in range(TJ):
                    pe.wait_ge(eo_ready, 4 * c + 3 + j // 2)
                    tile = slice(j * P, (j + 1) * P)
                    product(ps[:, MM_BANK + j, :],
                            [(xT[:, kc, tile], w_split[2][part][:, kc, :]) for part, xT in THREE for kc in range(KC)]).then_inc(v_ps, 1)
                    if not last and j >= 1:
                        if j == 1:
                            pe.wait_ge(ln_done, c + 2)
                        for k in range(j - 1, TJ if j == TJ - 1 else j):
                            transpose_tile(k, xn[:, k, :], TJ * c + k + 1)

            pe.wait_ge(ln_done, 1)
            for j in range(TJ):
                transpose_tile(j, xn[:, j, :])
            a_chunk(0, first=True)
            with pe.Fori(1, N_CH - 1) as c:
                a_chunk(c)
            a_chunk(N_CH - 1, last=True)

            pe.wait_ge(t_lo, TJ * N_CH)

            def score_bank(u, slot, uses, i, first=False):
                if i == 0:
                    pe.wait_ge(head_in[slot], 64 * uses)
                if i == M_ENTRY + RING and not first:
                    pe.wait_ge(max_T, u)
                elif i == M_ENTRY + RING:
                    pe.wait_ge(s_max, s_before(M_ENTRY - RING) + 1)
                elif i >= RING:
                    pe.wait_ge(s_max, NS * u + s_before(i - RING) + 1)
                elif not first:
                    pe.wait_ge(s_max, NS * u - RING + i + 1)
                col = 0
                for qt, k0, w, _ in S_BANKS[i]:
                    ins = pe.matmul(ps[:, S_BANK + i % RING, col:col + w], q_st[0:K_DOT, slot, qt * P:(qt + 1) * P],
                                    k_st[0:K_DOT, slot, k0:k0 + w], start=True, stop=True)
                    col += w
                ins.then_inc(s_ps, 1)

            def transpose_max(v, first=False, scores=True):
                pe.wait_ge(max_ready, v + 1)
                if scores:
                    pe.wait_ge(s_max, NS * (v + 1) + s_before(M_ENTRY - RING) + 1)
                if not first:
                    pe.wait_ge(max_T, v)
                pe.transpose(ps[0:2 * KT, M_BANK, 0:P], neg_max[:, :].bitcast(F32), ident[:, :]).then_inc(max_T_ps, 1)

            def shifted_piece(t, slot, uses, i, first=False):
                kt, q0, w, keep = ST_PIECES[i]
                if i == 0:
                    pe.wait_ge(max_in[slot], 32 * uses)
                if not (first and i < RING):
                    pe.wait_ge(exp_done, NPC * t + i - RING + 1)
                diagonal = i == 0 or ST_PIECES[i - 1][0] != kt
                dst = ps[:, ST_BANK + i % RING, :]
                ins = pe.matmul(dst[:, 0:w], k_st[0:K_ALL, slot, kt * P:(kt + 1) * P], q_st[0:K_ALL, slot, q0:q0 + w],
                                start=True, stop=not diagonal)
                if diagonal:
                    d0 = P * kt - q0
                    ins = pe.matmul(dst[:, d0:d0 + P], ident_b[:, :], mask_kq[:, :], start=False, stop=True)
                ins.then_inc(st_ps, 1)

            def output_products(r, half, i, first=False):
                for kt, qt, part in PV_TERMS[sum(PV_COUNTS[:i]):sum(PV_COUNTS[:i + 1])]:
                    if qt == kt and part == 0:
                        if kt not in split_of(r)["high"]:
                            pe.wait_ge(exp_done, NPC * r + LAST_PIECE[kt] + 1)
                        else:
                            pe.wait_ge(p_hi_dve, split_count("high", r, kt))
                        if kt in split_of(r)["pool"]:
                            pe.wait_ge(p_lo_pool, split_count("pool", r, kt))
                        else:
                            pe.wait_ge(p_lo_dve, split_count("low", r, kt))
                    opens = kt == 0 and qt % 4 == 0 and part == 0
                    if opens and not first:
                        pe.wait_ge(o_parts, 2 * r - 1 + qt // 4)
                    at = P_OFF[kt] + (qt - kt) * P
                    ins = pe.matmul(ps[:, O_BANK + qt // 4, qt % 4 * VW:(qt % 4 + 1) * VW], (p_hi, p_lo)[part][:, half, at:at + P],
                                    v_sb[:, kt, bass.ds(r, 1), 0:VW].rearrange("p o e -> p (o e)"),
                                    start=opens, stop=(part == 1 and kt == LAST_KEYS[qt]), skip_group_check=True)
                    if (kt, qt, part) in (PV_LAST_FIRST, PV_TERMS[-1]):
                        ins.then_inc(pv_done if qt >= KT // 2 else pv_first, 1)

            def tokens(c, j):
                b, cc = divmod(c, CC)
                return tok[:, cc * TJ + j, b, :]

            def b_step(t, j, it, scores=True, maxima=True, shifted=True, before=True):
                for i in range(NPC):
                    if not shifted and before and i == 7:
                        pe.wait_ge(o_done, NH)
                        pe.wait_ge(s_max, NS * HEADS)
                        pe.wait_ge(max_T, HEADS)
                        pe.wait_ge(exp_done, NPC * HEADS)
                        for k in range(TJ):
                            transpose_tile(k, tokens(0, k), TJ * N_CH)
                    if i == M_ENTRY and maxima:
                        transpose_max(t + 1, first=not shifted, scores=scores)
                    elif i != M_ENTRY and scores:
                        score_bank(t + 2, (j + 2) % SLOTS, it + (j + 2) // SLOTS + 1, i, first=not shifted and not maxima)
                    if shifted:
                        shifted_piece(t, j, it + 1, i, first=not before)
                    if before:
                        output_products(t - 1, (j + 1) % 2, i, first=(it == 0 and j == 1) if type(it) is int else False)

            b_step(-2, 2, -1, maxima=False, shifted=False, before=False)
            b_step(-1, 3, -1, shifted=False, before=False)
            pe.wait_ge(q_rows, 16)
            pe.wait_ge(k_rows, 16)
            pe.wait_ge(v32_ready, N_CH * TJ)
            pe.wait_ge(v2_ready, N_CH * TJ)
            pe.wait_ge(v3_ready, N_CH * TJ)
            for j in range(SLOTS):
                b_step(j, j, 0, before=j > 0)
            with pe.Fori(1, HEADS // SLOTS - 1) as it:
                for j in range(SLOTS):
                    b_step(it * SLOTS + j, j, it)
            for j in range(SLOTS + 1):
                t = HEADS - SLOTS + j
                b_step(t, j, HEADS // SLOTS - 1, scores=t + 2 < HEADS, maxima=t + 1 < HEADS, shifted=t < HEADS)

            pe.wait_ge(wo_lo_done, KC)

            def c2_tile(c, j):
                pe.wait_ge(x2_tokens, TJ * c + j + 1)
                transpose_tile(j, xst_c[:, j, :], TJ * (2 * N_CH + c), c2=True)

            for c in range(N_CH):
                for j in range(TJ):
                    if c == 0 and j == 2:
                        stage_b_done(pe)
                    tile = slice(j * P, (j + 1) * P)
                    if c > 0:
                        pe.wait_ge(x2_ready, TJ * (c - 1) + j + 1)
                    pe.wait_ge(t_lo, TJ * (N_CH + c) + j + 1)
                    product(ps[:, MM_BANK + j, :],
                            [(xT[:, kc, tile], (wo_hi, wo_lo)[part][:, kc, :]) for part, xT in THREE for kc in range(KC)]).then_inc(o_ps, 1)
                    if c + 1 < N_CH:
                        transpose_tile(j, tokens(c + 1, j), TJ * (N_CH + c) + j + 1)
                    else:
                        c2_tile(0, j)

            def ffn_products(dt):
                def t(ap):
                    return ap if dt == F32R else ap.bitcast(F32)

                pe.wait_ge(gate_in, 16)
                pe.wait_ge(up_in, 16)

                def gate_up(c, i):
                    n = IT * c + i
                    if i >= 2:
                        pe.wait_ge(hid_ready, n - 1)
                    cols = slice(i * P, (i + 1) * P)
                    for k, (w, done) in enumerate(((wg_sb, g_ps), (wu_sb, u_ps))):
                        product(ps[:, T_BANK + 2 * (i % 2) + k, :],
                                [(t(w[:, kc, cols]), t(xT[:, kc, :])) for kc in range(KC) for xT in (xT_hi, xT_lo)]).then_inc(done, 1)

                def down(c, i, first):
                    if i == 0 and first:
                        pe.wait_ge(x2_ready, TJ * N_CH)
                        pe.wait_ge(down_in, 16)
                    elif i == 0:
                        pe.wait_ge(y_scaled, TJ * c)
                    pe.wait_ge(hid_hi_done, IT * c + i + 1)
                    pe.wait_ge(hid_lo_done, IT * c + i + 1)
                    for j in range(TJ):
                        tile = slice(j * P, (j + 1) * P)
                        for k, h in enumerate((hid_hi, hid_lo)):
                            ins = pe.matmul(ps[:, MM_BANK + j, :], t(h[:, i % 3, tile]), t(wd_sb[:, i, :]),
                                            start=(i == 0 and k == 0), stop=(i == IT - 1 and k == 1))
                        if i == IT - 1 and j < TJ - 1:
                            ins.then_inc(y_ps, 1)
                    ins.then_inc(down_ps, 1)

                def c2_chunk(c, first=False, last=False):
                    pe.wait_ge(t_lo, TJ * (2 * N_CH + c + 1))
                    gate_up(c, 0)
                    for i in range(1, IT - 2):
                        gate_up(c, i)
                        down(c, i - 1, first)
                    gate_up(c, IT - 2)
                    gate_up(c, IT - 1)
                    for half in range(2):
                        if not last:
                            pe.wait_ge(hid_ready, IT * c + IT - 1 + half)
                            for j in range(2 * half, 2 * half + 2):
                                c2_tile(c + 1, j)
                        down(c, IT - 3 + half, first)
                    down(c, IT - 1, first)

                c2_chunk(0, first=True)
                with pe.Fori(1, N_CH - 1) as c:
                    c2_chunk(c)
                c2_chunk(N_CH - 1, last=True)

            pe.wait_ge(flag_ready, 2)
            inexact = pe.value_load(flag_int[0:1, 0:1])
            with pe.If(inexact == 0):
                ffn_products(F32R)
            with pe.Else():
                ffn_products(F32)


def kernel(L0_attn_x, L0_attn_Wq, L0_attn_bq, L0_attn_Wk, L0_attn_bk, L0_attn_Wv, L0_attn_bv, L0_attn_Wo, L0_attn_bo,
           L0_ffn_gate_w, L0_ffn_up_w, L0_ffn_down_w, L0_ffn_gate_s, L0_ffn_up_s, L0_ffn_down_s):
    import numpy as np
    import concourse.bacc as bacc
    from concourse.bass_utils import run_bass_kernel_spmd

    def rows_on_partitions(w):
        return np.ascontiguousarray(np.asarray(w).reshape(-1, P, w.shape[1]).transpose(1, 0, 2).reshape(P, -1))

    order = np.arange(H).reshape(2, HALF, D // 2, 2).transpose(0, 3, 1, 2).reshape(-1)

    def per_partition(v, n):
        return np.ascontiguousarray(np.asarray(v).reshape(n, P).T)

    inv_freq = (1.0 / np.float32(10000.0) ** (np.arange(D // 2, dtype=np.float32) / np.float32(D // 2))).astype(np.float32)
    freqs = np.arange(S, dtype=np.float32)[None, :] * inv_freq[:, None]
    wq, wk = np.asarray(L0_attn_Wq), np.asarray(L0_attn_Wk)
    arrays = {
        "x": np.ascontiguousarray(L0_attn_x),
        "wq": rows_on_partitions(wq[order].T), "wk": rows_on_partitions(wk[order].T),
        "wv": rows_on_partitions(np.asarray(L0_attn_Wv).T), "wo": rows_on_partitions(np.asarray(L0_attn_Wo).T),
        "bqk": np.concatenate([per_partition(np.asarray(v)[order], KC) for v in (L0_attn_bq, L0_attn_bk)], axis=1),
        "bv": np.ascontiguousarray(L0_attn_bv), "bo": np.ascontiguousarray(L0_attn_bo),
        "ffn": np.concatenate([rows_on_partitions(np.asarray(w).T) for w in (L0_ffn_gate_w, L0_ffn_up_w, L0_ffn_down_w)], axis=1),
        "gs": per_partition(L0_ffn_gate_s, IT), "us": per_partition(L0_ffn_up_s, IT), "ds": np.ascontiguousarray(L0_ffn_down_s),
        "cos": np.tile(np.cos(freqs).astype(np.float32), (HALF, 1)), "sin": np.tile(np.sin(freqs).astype(np.float32), (HALF, 1)),
        "shift_rows": np.concatenate([np.full((1, SLOTS * S), SHIFT, np.float32), np.ones((K_ALL - K_DOT, SLOTS * S), np.float32)]),
    }
    nc = bacc.Bacc("TRN2", target_bir_lowering=False, num_devices=1)
    aps = {k: nc.dram_tensor(f"in_{k}", v.shape, mybir.dt.from_np(v.dtype), kind="ExternalInput").ap() for k, v in arrays.items()}
    out = nc.dram_tensor("out", (NB, S, H), F32, kind="ExternalOutput").ap()
    transformer_block(nc, out=out, **aps)
    r = run_bass_kernel_spmd(nc, [{f"in_{k}": v for k, v in arrays.items()}], core_ids=[0])
    return r.results[0]["out"]
```
